# Optimizing a Trainium2 kernel written in Bass

```python
import numpy as np
import jax
import jax.numpy as jnp

def _softmax(x, axis=-1):
    return jax.nn.softmax(x, axis=axis)

def _gelu(x):
    return jax.nn.gelu(x, approximate=True)

def _silu(x):
    return jax.nn.silu(x)

def _sigmoid(x):
    return jax.nn.sigmoid(x)

def _layernorm(x, axis=-1, eps=1e-05):
    m = jnp.mean(x, axis=axis, keepdims=True)
    v = jnp.var(x, axis=axis, keepdims=True)
    return (x - m) / jnp.sqrt(v + eps)

def _scatter_add(tgt, idx, src, axis=0):
    return tgt.at[idx].add(src)

def _segment_sum(src, seg, n):
    return jax.ops.segment_sum(src, seg, n)
kernel_name = 'mk_seq_preln_d1_jaxref_r4_a450f1'

def setup_inputs(seed: int=0):
    np.random.seed(seed)
    _w = jnp.asarray

    def _L0_attn_setup():
        import jax, jax.numpy as jnp
        import numpy as np
        EPS = 1e-05

        def layer_norm(x, w, b):
            mu = jnp.mean(x, axis=-1, keepdims=True)
            var = jnp.var(x, axis=-1, keepdims=True)
            return (x - mu) / jnp.sqrt(var + EPS) * w + b
        key = jax.random.key(seed)
        B, N, C = (4, 1024, 256)
        H = 16
        MW = 4 * C
        ks = jax.random.split(key, 8)
        s = 0.02
        return {'x': jax.random.normal(ks[0], (B, N, C), dtype=jnp.float32), 'ln1_w': jnp.ones((C,), jnp.float32), 'ln1_b': jnp.zeros((C,), jnp.float32), 'q_w': jax.random.normal(ks[1], (C, C), jnp.float32) * s, 'q_b': jnp.zeros((C,), jnp.float32), 'k_w': jax.random.normal(ks[2], (C, C), jnp.float32) * s, 'k_b': jnp.zeros((C,), jnp.float32), 'v_w': jax.random.normal(ks[3], (C, C), jnp.float32) * s, 'v_b': jnp.zeros((C,), jnp.float32), 'o_w': jax.random.normal(ks[4], (C, C), jnp.float32) * s, 'o_b': jnp.zeros((C,), jnp.float32), 'ln2_w': jnp.ones((C,), jnp.float32), 'ln2_b': jnp.zeros((C,), jnp.float32), 'fc_w': jax.random.normal(ks[5], (MW, C), jnp.float32) * s, 'fc_b': jnp.zeros((MW,), jnp.float32), 'proj_w': jax.random.normal(ks[6], (C, MW), jnp.float32) * s, 'proj_b': jnp.zeros((C,), jnp.float32)}
    _L0_attn_in = _L0_attn_setup()

    def _L0_ffn_setup():
        import jax, jax.numpy as jnp
        import numpy as np
        HIDDEN = 256
        INTER = 1024
        key = jax.random.key(seed)
        k1, k2, k3, k4, k5 = jax.random.split(key, 5)
        hidden_states = jax.random.normal(k1, (4, 512, HIDDEN), dtype=jnp.float32)
        W1 = jax.random.normal(k2, (HIDDEN, INTER), dtype=jnp.float32) * (1.0 / np.sqrt(HIDDEN))
        b1 = jax.random.normal(k3, (INTER,), dtype=jnp.float32) * 0.02
        W2 = jax.random.normal(k4, (INTER, HIDDEN), dtype=jnp.float32) * (1.0 / np.sqrt(INTER))
        b2 = jax.random.normal(k5, (HIDDEN,), dtype=jnp.float32) * 0.02
        return {'hidden_states': hidden_states, 'W1': W1, 'b1': b1, 'W2': W2, 'b2': b2}
    _L0_ffn_in = _L0_ffn_setup()
    _d = {'L0_attn_x': _L0_attn_in['x'], 'L0_attn_ln1_w': _L0_attn_in['ln1_w'], 'L0_attn_ln1_b': _L0_attn_in['ln1_b'], 'L0_attn_q_w': _L0_attn_in['q_w'], 'L0_attn_q_b': _L0_attn_in['q_b'], 'L0_attn_k_w': _L0_attn_in['k_w'], 'L0_attn_k_b': _L0_attn_in['k_b'], 'L0_attn_v_w': _L0_attn_in['v_w'], 'L0_attn_v_b': _L0_attn_in['v_b'], 'L0_attn_o_w': _L0_attn_in['o_w'], 'L0_attn_o_b': _L0_attn_in['o_b'], 'L0_attn_ln2_w': _L0_attn_in['ln2_w'], 'L0_attn_ln2_b': _L0_attn_in['ln2_b'], 'L0_attn_fc_w': _L0_attn_in['fc_w'], 'L0_attn_fc_b': _L0_attn_in['fc_b'], 'L0_attn_proj_w': _L0_attn_in['proj_w'], 'L0_attn_proj_b': _L0_attn_in['proj_b'], 'L0_ffn_W1': _L0_ffn_in['W1'], 'L0_ffn_b1': _L0_ffn_in['b1'], 'L0_ffn_W2': _L0_ffn_in['W2'], 'L0_ffn_b2': _L0_ffn_in['b2']}
    _x0 = _d['L0_attn_x']
    _d['L0_attn_x'] = jax.random.normal(jax.random.fold_in(jax.random.key(seed), 1), (8, 1024, 256), dtype=_x0.dtype)
    del _x0
    return _d

def reference(L0_attn_x, L0_attn_ln1_w, L0_attn_ln1_b, L0_attn_q_w, L0_attn_q_b, L0_attn_k_w, L0_attn_k_b, L0_attn_v_w, L0_attn_v_b, L0_attn_o_w, L0_attn_o_b, L0_attn_ln2_w, L0_attn_ln2_b, L0_attn_fc_w, L0_attn_fc_b, L0_attn_proj_w, L0_attn_proj_b, L0_ffn_W1, L0_ffn_b1, L0_ffn_W2, L0_ffn_b2):

    def _L0_attn_ref(x, ln1_w, ln1_b, q_w, q_b, k_w, k_b, v_w, v_b, o_w, o_b, ln2_w, ln2_b, fc_w, fc_b, proj_w, proj_b):
        import jax, jax.numpy as jnp
        import numpy as np
        EPS = 1e-05

        def layer_norm(x, w, b):
            mu = jnp.mean(x, axis=-1, keepdims=True)
            var = jnp.var(x, axis=-1, keepdims=True)
            return (x - mu) / jnp.sqrt(var + EPS) * w + b
        B, N, C = x.shape
        H = 16
        D = C // H
        xn = layer_norm(x, ln1_w, ln1_b)
        q = (xn @ q_w.T + q_b).reshape(B, N, H, D).transpose(0, 2, 1, 3)
        k = (xn @ k_w.T + k_b).reshape(B, N, H, D).transpose(0, 2, 1, 3)
        v = (xn @ v_w.T + v_b).reshape(B, N, H, D).transpose(0, 2, 1, 3)
        q = jax.nn.elu(q) + 1.0
        k = jax.nn.elu(k) + 1.0
        kv = jnp.einsum('bhnd,bhne->bnde', k, v)
        qkv = jnp.einsum('bhnd,bnde->bhne', q, kv)
        k_sum = k.sum(axis=1)
        qk = jnp.einsum('bhnd,bnd->bhn', q, k_sum)
        attn = qkv / qk[..., None]
        attn = attn.transpose(0, 2, 1, 3).reshape(B, N, C)
        attn = attn @ o_w.T + o_b
        x = x + attn
        xn2 = layer_norm(x, ln2_w, ln2_b)
        h = jax.nn.gelu(xn2 @ fc_w.T + fc_b, approximate=False)
        x = x + (h @ proj_w.T + proj_b)
        return x

    def _L0_ffn_ref(hidden_states, W1, b1, W2, b2):
        import jax, jax.numpy as jnp
        import numpy as np
        HIDDEN = 256
        INTER = 1024
        h = jax.nn.relu(jnp.einsum('bsh,hi->bsi', hidden_states, W1) + b1)
        return jnp.einsum('bsi,ih->bsh', h, W2) + b2
    x = L0_attn_x
    x = x + _L0_attn_ref(_layernorm(x, axis=-1), L0_attn_ln1_w, L0_attn_ln1_b, L0_attn_q_w, L0_attn_q_b, L0_attn_k_w, L0_attn_k_b, L0_attn_v_w, L0_attn_v_b, L0_attn_o_w, L0_attn_o_b, L0_attn_ln2_w, L0_attn_ln2_b, L0_attn_fc_w, L0_attn_fc_b, L0_attn_proj_w, L0_attn_proj_b)
    x = x + _L0_ffn_ref(_layernorm(x, axis=-1), L0_ffn_W1, L0_ffn_b1, L0_ffn_W2, L0_ffn_b2)
    return x

_drawn_inputs = setup_inputs


def setup_inputs(seed=0):
    import zlib

    import numpy as np

    out = dict(_drawn_inputs(seed))
    spreads = {'L0_attn_ln1_w': (1.0, 0.6),
     'L0_attn_ln1_b': (0.0, 0.8),
     'L0_attn_q_b': (0.0, 2.0),
     'L0_attn_k_b': (0.0, 0.8),
     'L0_attn_v_b': (0.0, 0.8),
     'L0_attn_o_b': (0.0, 0.1),
     'L0_attn_ln2_w': (1.0, 0.6),
     'L0_attn_ln2_b': (0.0, 0.8),
     'L0_attn_fc_b': (0.0, 0.464),
     'L0_attn_proj_b': (0.0, 0.1)}
    factors = {'L0_attn_q_w': 8.0,
     'L0_attn_k_w': 8.0,
     'L0_attn_v_w': 4.232,
     'L0_attn_o_w': 4.007,
     'L0_ffn_b1': 8.0,
     'L0_ffn_b2': 6.186}
    for name, (base, spread) in spreads.items():
        noise = np.random.default_rng([zlib.crc32(name.encode()), seed]).standard_normal(out[name].shape)
        drawn = base * np.exp(spread * noise) if base else spread * noise
        out[name] = jnp.asarray(drawn.astype(out[name].dtype))
    for name, factor in factors.items():
        out[name] = (out[name] * factor).astype(out[name].dtype)
    return out
```

```python
from contextlib import ExitStack

import concourse.bass as bass
from concourse import mybir

F32 = mybir.dt.float32
F32R = mybir.dt.float32r
ALU = mybir.AluOpType
ACT = mybir.ActivationFunctionType

P = 128
T = 8192
C = 256
KC = C // P
F = 1024
FB = F // P
H, D = 16, 16
TT = 256
TA = TT // P
NT = T // TT
CH = P // H
NCH = P // CH
EPS = 1e-5
DEPTH = 5


def after(eng, *needs, own=False):
    values = []
    for sem, tile, k, per in needs:
        if isinstance(tile, int):
            if tile >= 0:
                values.append((sem, min(tile, NT - 1) * per + (k if tile < NT else per)))
        else:
            values.append((sem, eng.snap(tile * per + k)))
    for sem, value in values:
        eng.wait_ge(sem, value)
        if own and not isinstance(value, int):
            eng.nop(nofuse=True)


def live(tile):
    return not isinstance(tile, int) or 0 <= tile < NT


def run(eng, body):
    for i in range(DEPTH + 1):
        body(i, True)
    with eng.Fori(DEPTH + 1, NT) as i:
        body(i, False)
    for i in range(NT, NT + DEPTH):
        body(i, True)


def build(nc, x, wqkv, bqkv, ln1w, ln1b, wo, bo, ln2w, ln2b, wfc, bfc, wproj, bproj, w1, b1, w2, b2, ident_in, mask_in, out):
    with ExitStack() as ctx:
        def sb(name, shape, dt=F32):
            return ctx.enter_context(nc.sbuf_tensor(name, shape, dt))

        def sem(name):
            return ctx.enter_context(nc.semaphore(name))

        WQKV = [sb(f"wqkv_{p}", [P, KC, 3 * C], F32R) for p in "hl"]
        WO = [sb(f"wo_{p}", [P, KC, C], F32R) for p in "hl"]
        WFC = [sb(f"wfc_{p}", [P, KC, F], F32R) for p in "hl"]
        WPROJ = [sb(f"wproj_{p}", [P, FB, C], F32R) for p in "hl"]
        W1 = [sb(f"w1_{p}", [P, KC, F], F32R) for p in "hl"]
        W2 = [sb(f"w2_{p}", [P, FB, C], F32R) for p in "hl"]
        ident = sb("ident", [P, P])
        mask = sb("mask", [P, P])
        bqkv_raw = sb("bqkv_raw", [P, 6])
        bfc_raw = sb("bfc_raw", [P, FB])
        qkv_bias = sb("qkv_bias", [P, 6])
        fc_bias = sb("fc_bias", [P, FB])
        b1_sb = sb("b1_sb", [P, FB])
        ln1 = sb("ln1", [P, 2, KC])
        ln2 = sb("ln2", [P, 2, KC])
        bo_rows = sb("bo_rows", [P, C])
        bproj_rows = sb("bproj_rows", [P, C])
        b2_rows = sb("b2_rows", [P, C])
        minus_half = sb("minus_half", [P, TA])
        X = sb("X", [P, TA, C])
        XC = sb("XC", [P, TA, C])
        Y = sb("Y", [P, TA, C])
        X2 = sb("X2", [P, TA, C])
        RES = sb("RES", [P, TA, C])
        X3 = sb("X3", [P, TA, C])
        Z3 = sb("Z3", [P, TA, C])
        X3B = sb("X3B", [P, TA, C])
        OUTB = sb("OUTB", [P, TA, C])
        ZT = [sb(f"zt_{p}", [P, KC, TT], F32R) for p in "hl"]
        Z2T = [sb(f"z2t_{p}", [P, KC, TT], F32R) for p in "hl"]
        Z3T = [sb(f"z3t_{p}", [P, KC, TT], F32R) for p in "hl"]
        HB = [sb(f"hidden_{p}", [P, FB, TT], F32R) for p in "hl"]
        HF = sb("hidden_f32", [P, 2, 2 * TT])
        EXPRELU = sb("exp_relu", [P, 4, TA * KC * P])
        QKH = [sb(f"{n}_hi", [P, TA, KC * P], F32R) for n in "qk"]
        QKL = [sb(f"{n}_lo", [P, TA, KC * P], F32R) for n in "qk"]
        VN = sb("VN", [P, TA, KC * P])
        QD = sb("QD", [P, H * P], F32R)
        KD = sb("KD", [P, H * P], F32R)
        VD = sb("VD", [P, H * P])
        VC = sb("VC", [P, TA * NCH, 2 * D])
        A = sb("A", [P, 4, 4 * P])
        ND = sb("ND", [P, H, 8, 8])
        NN = sb("NN", [P, 4, 2, 64])
        DD = sb("DD", [P, 4, 2, 64])
        AT = sb("AT", [P, TA, KC, P])
        ATH = sb("AT_hi", [P, TA, KC, P], F32R)
        ATL = sb("AT_lo", [P, TA, KC, P], F32R)
        bn = {n: sb(f"bn_{n}", [P, TA, 6]) for n in ("x", "xc", "x2", "x3")}
        mv = {n: sb(f"mv_{n}", [P, TA, 2]) for n in ("x", "xc", "x2", "x3")}
        ve = {n: sb(f"ve_{n}", [P, TA]) for n in ("x", "xc", "x2", "x3")}
        rs = {n: sb(f"rs_{n}", [P, TA]) for n in ("x", "xc", "x2", "x3")}
        sq = sb("sq", [P, TA])
        sv = sb("sv", [P, TA])
        se = sb("se", [P, TA])
        rz1 = sb("rz1", [P, TA])
        rz = sb("rz", [P, TA])

        def bank(name):
            return ctx.enter_context(nc.psum_tensor(name, [P, 512], F32))
        turn = bank("turn")
        wide = [bank("wide_a"), bank("wide_b")]
        rows = bank("rows")
        score = [bank("score_0"), bank("score_1")]
        summed = [bank("summed_0"), bank("summed_1")]

        const_loaded = sem("const_loaded")
        w_loaded = [sem(f"w_loaded_{n}") for n in range(6)]
        w_scaled, w_hi, w_lo, w_bias_sum, w_bias = (sem(n) for n in ("w_scaled", "w_hi", "w_lo", "w_bias_sum", "w_bias"))
        ones_set = sem("ones_set")
        x_loaded = sem("x_loaded")
        xc_loaded = sem("xc_loaded")
        bn_done = {n: sem(f"bn_done_{n}") for n in bn}
        stats = {n: sem(f"stats_{n}") for n in bn}
        scale = {n: sem(f"scale_{n}") for n in bn}
        z_ready, z2_ready, z3_ready = sem("z_ready"), sem("z2_ready"), sem("z3_ready")
        z_turned, z2_turned, z3_turned = sem("z_turned"), sem("z2_turned"), sem("z3_turned")
        zh, z2h, z3h = sem("zh"), sem("z2h"), sem("z3h")
        zl, z2l, z3l = sem("zl"), sem("z2l"), sem("z3l")
        vqk_ready = sem("vqk_ready")
        qk_act = sem("qk_act")
        v_act = sem("v_act")
        qk_made = sem("qk_made")
        qk_hi = sem("qk_hi")
        qk_lo = sem("qk_lo")
        q_moved, k_moved = sem("q_moved"), sem("k_moved")
        v_moved = sem("v_moved")
        v_turned = sem("v_turned")
        vc_ready = sem("vc_ready")
        scored = sem("scored")
        masked = sem("masked")
        a_used = sem("a_used")
        nd_ready = sem("nd_ready")
        num_moved, den_moved = sem("num_moved"), sem("den_moved")
        den_inverted = sem("den_inverted")
        at_made = sem("at_made")
        at_hi, at_lo = sem("at_hi"), sem("at_lo")
        y_ready, yb_ready = sem("y_ready"), sem("yb_ready")
        xc_biased = sem("xc_biased")
        o_ready, x2_ready, res_ready = sem("o_ready"), sem("x2_ready"), sem("res_ready")
        fc_ready, gelu_made, h_hi, h_lo = sem("fc_ready"), sem("gelu_made"), sem("h_hi"), sem("h_lo")
        proj_ready, x3_ready, x3b_ready = sem("proj_ready"), sem("x3_ready"), sem("x3b_ready")
        w1_ready, relu_made, g_hi, g_lo = sem("w1_ready"), sem("relu_made"), sem("g_hi"), sem("g_lo")
        w2_ready, out_ready = sem("w2_ready"), sem("out_ready")
        stored = sem("stored")

        x_rows = x.rearrange("(n p a) c -> n p (a c)", p=P, a=TA)
        x_rows_c = x.rearrange("(n s jj i a) c -> n jj s i (a c)", s=8, jj=2, i=8, a=TA)
        out_rows_c = out.rearrange("(n s jj i a) c -> n jj s i (a c)", s=8, jj=2, i=8, a=TA)

        stage_v = VD[:, :]
        stage_a = A[:, :, :].rearrange("p b n -> p (b n)")
        stage_e = EXPRELU[:, :, :].rearrange("p b n -> p (b n)")
        WEIGHTS = [
            (wqkv, stage_v, KC, 3 * C, WQKV, ln1), (wfc, stage_a, KC, F, WFC, ln2),
            (wproj, stage_e, FB, C, WPROJ, None), (w1, stage_v, KC, F, W1, None),
            (w2, stage_a, FB, C, W2, None), (wo, stage_e, KC, C, WO, None),
        ]

        def staged(n):
            _, stage, blocks, width, _, _ = WEIGHTS[n]
            return stage[:, 0:blocks * width].rearrange("p (k n) -> p k n", k=blocks)

        block = ctx.enter_context(nc.Block())

        @block.sync
        def _(sp):
            consts = [(ident[:], ident_in), (mask[:], mask_in), (ln1[:, 0, :], ln1w), (ln1[:, 1, :], ln1b),
                      (ln2[:, 0, :], ln2w), (ln2[:, 1, :], ln2b), (bqkv_raw[:], bqkv), (bfc_raw[:], bfc), (b1_sb[:], b1),
                      (bo_rows[:], bo.partition_broadcast(P)), (bproj_rows[:], bproj.partition_broadcast(P)),
                      (b2_rows[:], b2.partition_broadcast(P))]
            for n, (source, _, _, _, _, _) in enumerate(WEIGHTS):
                if n == 1:
                    for dst, src in consts:
                        sp.dma_start(dst, src).then_inc(const_loaded, 16)
                if n >= 3:
                    sp.wait_ge(w_lo, n - 2)
                if n == 3:
                    sp.wait_ge(w_bias_sum, 1)
                if n == 4:
                    sp.wait_ge(w_bias_sum, 2)
                sp.dma_start(staged(n), source.rearrange("(k p) n -> p k n", p=P)).then_inc(w_loaded[n], 16)
            sp.wait_ge(const_loaded, 16 * len(consts))

            def body(i, peeled):
                a, q, c, e = i, i - 1, i - 2, i - 5
                if live(c):
                    after(sp, (res_ready, c - 1, 1, 1), own=True)
                    for jj in range(2):
                        sp.dma_start(XC[64 * jj:64 * jj + 64, :, :].rearrange("p a c -> p (a c)"),
                                     x_rows_c[c, jj]).then_inc(xc_loaded, 16)
                if live(a):
                    after(sp, (z_turned, a - 1, 1, 1), own=True)
                    sp.dma_start(X[:, :, :].rearrange("p a c -> p (a c)"), x_rows[a]).then_inc(x_loaded, 16)
                if live(e):
                    after(sp, (out_ready, e, 1, 1), own=True)
                    for jj in range(2):
                        sp.dma_start(out_rows_c[e, jj],
                                     OUTB[64 * jj:64 * jj + 64, :, :].rearrange("p a c -> p (a c)")).then_inc(stored, 16)
                if live(c):
                    after(sp, (nd_ready, c, 2, 2), (at_made, c - 1, 2, 2), own=True)
                    for dst, part, moved in ((DD, D, den_moved), (NN, 0, num_moved)):
                        for j in range(4):
                            sp.dma_start(dst[:, j, :, :].rearrange("p m t -> p (m t)"),
                                         ND[32 * j + part:32 * j + part + D, :, :, :].rearrange("p h s i -> p (h s i)"))\
                              .then_inc(moved, 16)
                if live(q):
                    after(sp, (v_act, q, 1, 1), (v_turned, q - 1, 1, 1), own=True)
                    for g in range(TA):
                        sp.dma_start(VD[D * g:D * g + D, :], VN[:, g, :]).then_inc(v_moved, 16)
                    after(sp, (scored, q - 1, 8, 8), own=True)
                    for t, (dst, his, moved) in enumerate(((QD, (0, 2), q_moved), (KD, (0, 1), k_moved))):
                        after(sp, (qk_hi, q, t + 1, 2), own=True)
                        for g in range(TA):
                            for h in his:
                                sp.dma_start(dst[64 * g + D * h:64 * g + D * h + D, :].bitcast(F32),
                                             QKH[t][:, g, :].bitcast(F32)).then_inc(moved, 16)
                    for t, (dst, lo, moved) in enumerate(((QD, 1, q_moved), (KD, 2, k_moved))):
                        after(sp, (qk_lo, q, t + 1, 2), own=True)
                        for g in range(TA):
                            sp.dma_start(dst[64 * g + D * lo:64 * g + D * lo + D, :].bitcast(F32),
                                         QKL[t][:, g, :].bitcast(F32)).then_inc(moved, 16)

            run(sp, body)
            sp.wait_ge(stored, 32 * NT)

        @block.tensor
        def _(pe):
            pe.wait_ge(const_loaded, 16 * 12)
            for n, (b, ln, blocks) in enumerate(((wide[0], ln1, 6), (wide[1], ln2, FB))):
                pe.wait_ge(w_loaded[n], 16)
                for m in range(blocks):
                    for k in range(KC):
                        mm = pe.matmul(b[:, m:m + 1], staged(n)[:, k, P * m:P * m + P], ln[:, 1, k:k + 1],
                                       start=(k == 0), stop=(k == KC - 1))
                mm.then_inc(w_bias_sum, 1)
            pe.wait_ge(w_lo, 6)
            pe.wait_ge(w_bias, 2)

            def product(dst, hi_lo_w, hi_lo_x, parts, last_sem=None):
                passes = [(0, 0), (1, 0), (0, 1)]
                n = len(parts)
                for k, (w, xx) in enumerate(parts):
                    for m, (pw, px) in enumerate(passes):
                        mm = pe.matmul(dst, w(hi_lo_w[pw]), xx(hi_lo_x[px]), start=(k == 0 and m == 0),
                                       stop=(k == n - 1 and m == 2))
                return mm

            def turn_rows(z):
                for g in range(TA):
                    for k in range(KC):
                        mm = pe.transpose(turn[:, TT * k + P * g:TT * k + P * g + P], z[:, g, P * k:P * k + P], ident[:])
                return mm

            def blocks_of(w, zt, first, dst):
                for b in range(2):
                    lo = P * (first + b)
                    mm = product(dst[:, TT * b:TT * b + TT], w, zt,
                                 [(lambda v, k=k: v[:, k, lo:lo + P], lambda v, k=k: v[:, k, :]) for k in range(KC)])
                return mm

            def token_rows(act, w, count, wait_block=None, groups=range(TA)):
                for g in groups:
                    dst = rows[:, C * g:C * g + C]
                    for k in range(count):
                        if wait_block and g == 0:
                            wait_block(k)
                        for m, (pa, pw) in enumerate([(0, 0), (1, 0), (0, 1)]):
                            mm = pe.matmul(dst, act(pa, k, g), w[pw][:, k, :], start=(k == 0 and m == 0),
                                           stop=(k == count - 1 and m == 2))
                return mm

            def chunks(n):
                g, k = n % 2, n // 2
                for c, i in enumerate((2 * k, 2 * k + 1, 8 + 2 * k, 8 + 2 * k + 1)):
                    yield g, c, i, 2 * g + i // 8, i % 4

            def body(i, peeled):
                q, b, m, f, e = i - 1, i - 2, i - 3, i - 4, i - 5

                def scores(n):
                    if n == 0:
                        after(pe, (q_moved, b, 96, 96), (k_moved, b, 96, 96), (masked, b - 1, 7, 8))
                    elif n == 1:
                        after(pe, (masked, b - 1, 8, 8))
                    else:
                        after(pe, (masked, b, n - 1, 8))
                    for g, c, ch, _, _ in chunks(n):
                        mm = pe.matmul(score[g][:, P * c:P * c + P], KD[64 * g:64 * g + 3 * D, ch:H * P:NCH],
                                       QD[64 * g:64 * g + 3 * D, ch:H * P:NCH], start=True, stop=True)
                    mm.then_inc(scored, 1)

                def weighted(n):
                    if n == 0:
                        after(pe, (vc_ready, b, 1, 1), (masked, b, 1, 8), (nd_ready, b - 1, 1, 2))
                    elif n == 4:
                        after(pe, (masked, b, 5, 8), (nd_ready, b - 1, 2, 2))
                    else:
                        after(pe, (masked, b, n + 1, 8))
                    for g, c, ch, j, place in chunks(n):
                        mm = pe.matmul(summed[n // 4][32 * j:32 * j + 32, P * place:P * place + P], VC[:, NCH * g + ch, :],
                                       A[:, n % 4, P * c:P * c + P], start=True, stop=True)
                    mm.then_inc(a_used, 1)

                def turn_z2():
                    extra = [(z3l, f - 1, 1, 1)] if peeled else []
                    after(pe, (z2_ready, m, 1, 1), (vc_ready, b, 1, 1), *extra)
                    turn_rows(X2).then_inc(z2_turned, 1)

                def attend(*steps):
                    if live(b):
                        for n in steps:
                            weighted(n)
                            if n + 2 < 8:
                                scores(n + 2)

                for g in range(TA):
                    if live(e):
                        if g == 0:
                            extra = [(x3_ready, m - 1, 1, 1), (out_ready, e - 1, 1, 1)] if peeled else []
                            after(pe, (x2_ready, b - 1, 1, 1), *extra)

                        def g_block(k):
                            if k % 2 == 0:
                                after(pe, (g_lo, e, k // 2 + 1, 4))
                        mm = token_rows(lambda part, k, g: HB[part][:, k, P * g:P * g + P], W2, FB, g_block, [g])
                        if g == TA - 1:
                            mm.then_inc(w2_ready, 1)
                    if g == 0 and live(b):
                        scores(0)
                        scores(1)
                if live(m):
                    turn_z2()
                attend(0, 1, 2)
                if live(q):
                    extra = [(vc_ready, q - 1, 1, 1)] if peeled else []
                    after(pe, (z_ready, q, 1, 1), (z2l, m, 1, 1), *extra)
                    turn_rows(X).then_inc(z_turned, 1)
                for n, steps in enumerate(((3,), (4,), (5, 6), (7,))):
                    if live(m):
                        if n == 0:
                            extra = [(qk_act, q - 1, 2, 2), (gelu_made, m - 1, 4, 4)] if peeled else []
                            after(pe, (z2l, m, 1, 1), (relu_made, f - 1, 4, 4), *extra)
                        elif n >= 2:
                            after(pe, (gelu_made, m, n - 1, 4))
                        blocks_of(WFC, Z2T, 2 * n, wide[n % 2]).then_inc(fc_ready, 1)
                    attend(*steps)
                if live(f):
                    extra = [(z2l, m, 1, 1), (z3l, f - 1, 1, 1)] if peeled else []
                    after(pe, (z3_ready, f, 1, 1), (zl, q, 1, 1), *extra)
                    turn_rows(Z3).then_inc(z3_turned, 1)
                if live(q):
                    for n, t in enumerate((2, 0, 1)):
                        if n == 0:
                            extra = [(qk_act, q - 1, 2, 2)] if peeled else []
                            after(pe, (zl, q, 1, 1), (gelu_made, m, 3, 4), *extra)
                        elif n == 1:
                            after(pe, (gelu_made, m, 4, 4))
                        else:
                            after(pe, (v_act, q, 1, 1))
                        blocks_of(WQKV, ZT, 2 * t, wide[n % 2]).then_inc(vqk_ready, 1)
                if live(m):
                    extra = [(x2_ready, b - 1, 1, 1)] if peeled else []
                    after(pe, (out_ready, e, 1, 1), *extra)

                    def h_block(k):
                        if k % 2 == 0:
                            after(pe, (h_lo, m, k // 2 + 1, 4))
                    token_rows(lambda part, k, g: HB[part][:, k, P * g:P * g + P], WPROJ, FB, h_block).then_inc(proj_ready, 1)
                if live(f):
                    for n in range(4):
                        if n == 0:
                            extra = [(gelu_made, m, 4, 4), (relu_made, f - 1, 4, 4)] if peeled else []
                            after(pe, (z3l, f, 1, 1), (qk_act, q, 1, 2), *extra)
                        elif n == 1:
                            after(pe, (qk_act, q, 2, 2))
                        else:
                            after(pe, (relu_made, f, n - 1, 4))
                        blocks_of(W1, Z3T, 2 * n, wide[(n + 1) % 2]).then_inc(w1_ready, 1)
                if live(b):
                    after(pe, (at_hi, b, 1, 1), (at_lo, b, 1, 1), (x3_ready, m, 1, 1))
                    token_rows(lambda part, k, g: (ATH, ATL)[part][:, g, k, :], WO, KC).then_inc(o_ready, 1)
                if live(q):
                    extra = [(zl, q, 1, 1)] if peeled else []
                    after(pe, (v_moved, q, 32, 32), (z3l, f, 1, 1), *extra, own=True)
                    for ch in range(NCH):
                        mm = pe.transpose(turn[:, TA * D * ch:TA * D * ch + TA * D], VD[0:TA * D, ch:H * P:NCH],
                                          ident[0:TA * D, 0:TA * D])
                    mm.then_inc(v_turned, 1)

            run(pe, body)

        @block.scalar
        def _(act):
            for n, (_, _, _, _, w, ln) in enumerate(WEIGHTS):
                act.wait_ge(w_loaded[n], 16)
                if ln is not None:
                    act.wait_ge(w_scaled, n + 1)
                act.activation(w[0][:], staged(n), ACT.Copy).then_inc(w_hi, 1)
            act.wait_ge(w_bias, 2)
            act.wait_ge(const_loaded, 16 * 12)

            def body(i, peeled):
                q, b, m, f = i - 1, i - 2, i - 3, i - 4

                def sums(u):
                    after(act, (a_used, b, 4 * u + 4, 8), *([(num_moved, b - 1, 64, 64), (den_moved, b - 1, 64, 64)] if u == 0 else []))
                    act.activation(ND[:, :, :, 4 * u:4 * u + 4].rearrange("p h s i -> p i h s"),
                                   summed[u][:, :].rearrange("p (i h s) -> p i h s", i=4, h=H), ACT.Copy).then_inc(nd_ready, 1)

                def hi_part(dst, turned, tile, readers, signal):
                    after(act, (turned, tile, 1, 1), *readers)
                    act.activation(dst[:, :, :].rearrange("p k t -> p (k t)"), turn[:, :], ACT.Copy).then_inc(signal, 1)

                def hidden_hi(tile, n, made, readers, signal):
                    after(act, (made, tile, n + 1, 4), *(readers if n == 0 else []))
                    act.activation(HB[0][:, 2 * n:2 * n + 2, :].rearrange("p k t -> p (k t)"), HF[:, n % 2, :],
                                   ACT.Copy).then_inc(signal, 1)

                if live(m):
                    hi_part(Z2T[0], z2_turned, m, [(fc_ready, m - 1, 4, 4)], z2h)
                if live(q):
                    hi_part(ZT[0], z_turned, q, [(vqk_ready, q - 1, 3, 3)], zh)
                for n in range(4):
                    if live(m):
                        extra = [(h_lo, m - 1, 4, 4)] if peeled and n < 2 else []
                        free = (g_lo, f - 1, 4, 4) if n < 2 else (h_lo, m, n - 1, 4)
                        after(act, (fc_ready, m, n + 1, 4), free, *extra)
                        for k in range(2):
                            ins = act.activation(HF[:, n % 2, TT * k:TT * k + TT], wide[n % 2][:, TT * k:TT * k + TT], ACT.Gelu,
                                                 bias=fc_bias[:, 2 * n + k:2 * n + k + 1])
                        ins.then_inc(gelu_made, 1)
                        extra = [(proj_ready, m - 1, 1, 1)] if peeled else []
                        hidden_hi(m, n, gelu_made, [(w2_ready, f - 1, 1, 1), *extra], h_hi)
                    if live(b) and n in (2, 3):
                        sums(n - 2)
                if live(q):
                    after(act, (vqk_ready, q, 1, 3), (v_moved, q - 1, 32, 32))
                    for k in range(KC):
                        ins = act.activation(VN[:, :, :].rearrange("p g (m t) -> p g m t", m=KC)[:, :, k, :],
                                             wide[0][:, TT * k:TT * k + TT].rearrange("p (g t) -> p g t", g=TA), ACT.Identity,
                                             bias=qkv_bias[:, 4 + k:5 + k])
                    ins.then_inc(v_act, 1)
                if live(f):
                    hi_part(Z3T[0], z3_turned, f, [(w1_ready, f - 1, 4, 4)], z3h)
                if live(q):
                    for t in range(2):
                        after(act, (vqk_ready, q, t + 2, 3), (qk_lo, q - 1, t + 1, 2))
                        for s, fn in ((0, ACT.Exp), (2, ACT.Relu)):
                            for k in range(KC):
                                ins = act.activation(
                                    EXPRELU[:, t + s, :].rearrange("p (g m t) -> p g m t", g=TA, m=KC)[:, :, k, :],
                                    wide[(t + 1) % 2][:, TT * k:TT * k + TT].rearrange("p (g t) -> p g t", g=TA), fn,
                                    bias=qkv_bias[:, 2 * t + k:2 * t + k + 1])
                        ins.then_inc(qk_act, 1)
                    for t, moved in enumerate((q_moved, k_moved)):
                        after(act, (qk_made, q, t + 1, 2), (moved, q - 1, 96, 96))
                        act.activation(QKH[t][:, :, :].rearrange("p g n -> p (g n)"), EXPRELU[:, t, :], ACT.Copy).then_inc(qk_hi, 1)
                for n in range(4):
                    if live(f):
                        extra = [(g_lo, f - 1, 4, 4)] if peeled and n < 2 else []
                        free = (h_lo, m, n + 3, 4) if n < 2 else (g_lo, f, n - 1, 4)
                        after(act, (w1_ready, f, n + 1, 4), free, *extra)
                        for k in range(2):
                            ins = act.activation(HF[:, n % 2, TT * k:TT * k + TT], wide[(n + 1) % 2][:, TT * k:TT * k + TT], ACT.Relu,
                                                 bias=b1_sb[:, 2 * n + k:2 * n + k + 1])
                        ins.then_inc(relu_made, 1)
                    if live(b) and n == 1:
                        after(act, (at_made, b, 2, 2), (o_ready, b - 1, 1, 1))
                        act.activation(ATH[:, :, :, :].rearrange("p g m t -> p (g m t)"),
                                       AT[:, :, :, :].rearrange("p g m t -> p (g m t)"), ACT.Copy).then_inc(at_hi, 1)
                    if live(f):
                        extra = [(w2_ready, f - 1, 1, 1)] if peeled else []
                        hidden_hi(f, n, relu_made, [(proj_ready, m, 1, 1), *extra], g_hi)
                if live(q):
                    after(act, (v_turned, q, 1, 1), (a_used, q - 1, 8, 8))
                    act.activation(VC[:, :, 0:D].rearrange("p (g c) e -> p c g e", g=TA),
                                   turn[:, :].rearrange("p (c g e) -> p c g e", g=TA, e=D), ACT.Copy).then_inc(vc_ready, 1)

            run(act, body)

        @block.gpsimd
        def _(pool):
            pool.memset(minus_half[:], -0.5).then_inc(ones_set, 1)
            pool.memset(VC[:, :, D:2 * D], 1.0).then_inc(ones_set, 1)
            pool.wait_ge(const_loaded, 16 * 12)
            pool.wait_ge(ones_set, 2)

            def body(i, peeled):
                a, b, m, f = i, i - 2, i - 3, i - 4

                def inverse_root(n, tile, per):
                    after(pool, (stats[n], tile, 1, 1), own=True)
                    pool.tensor_scalar(ve[n][:], mv[n][:, :, 1], EPS, None, ALU.add).then_inc(scale[n], 1)
                    after(pool, (scale[n], tile, 1, per), own=True)
                    pool.tensor_tensor(rs[n][:], ve[n][:], minus_half[:], ALU.pow).then_inc(scale[n], 1)

                if live(b):
                    inverse_root("xc", b, 2)
                    after(pool, (y_ready, b, 1, 1), own=True)
                    for g in range(TA):
                        ins = pool.tensor_tensor(Y[:, g, :], Y[:, g, :], bo_rows[:], ALU.add)
                    ins.then_inc(yb_ready, 1)
                    for g in range(TA):
                        ins = pool.tensor_tensor(XC[:, g, :], XC[:, g, :], bproj_rows[:], ALU.add)
                    ins.then_inc(xc_biased, 1)
                if live(a):
                    inverse_root("x", a, 7)
                    after(pool, (scale["x"], a, 2, 7), own=True)
                    pool.tensor_tensor(sq[:], rs["x"][:], rs["x"][:], ALU.mult).then_inc(scale["x"], 1)
                    after(pool, (scale["x"], a, 3, 7), own=True)
                    pool.tensor_tensor(sv[:], sq[:], mv["x"][:, :, 1], ALU.mult).then_inc(scale["x"], 1)
                    after(pool, (scale["x"], a, 4, 7), own=True)
                    pool.tensor_scalar(se[:], sv[:], EPS, None, ALU.add).then_inc(scale["x"], 1)
                    after(pool, (scale["x"], a, 5, 7), own=True)
                    pool.tensor_tensor(rz1[:], se[:], minus_half[:], ALU.pow).then_inc(scale["x"], 1)
                    after(pool, (scale["x"], a, 6, 7), own=True)
                    pool.tensor_tensor(rz[:], rz1[:], rs["x"][:], ALU.mult).then_inc(scale["x"], 1)
                if live(b):
                    inverse_root("x2", b, 2)
                    after(pool, (x2_ready, b, 1, 1), (xc_biased, b, 1, 1), (x3_ready, m, 1, 1), own=True)
                    pool.tensor_tensor(RES[:].rearrange("p a c -> p (a c)"), X2[:].rearrange("p a c -> p (a c)"),
                                       XC[:].rearrange("p a c -> p (a c)"), ALU.add).then_inc(res_ready, 1)
                if live(m):
                    inverse_root("x3", m, 2)
                if live(m):
                    after(pool, (x3_ready, m, 1, 1), (out_ready, f, 1, 1), own=True)
                    for g in range(TA):
                        ins = pool.tensor_tensor(X3B[:, g, :], X3[:, g, :], b2_rows[:], ALU.add)
                    ins.then_inc(x3b_ready, 1)

            run(pool, body)

        @block.vector
        def _(dve):
            dve.wait_ge(const_loaded, 16 * 12)
            for n, (_, _, blocks, width, w, ln) in enumerate(WEIGHTS):
                dve.wait_ge(w_loaded[n], 16)
                if ln is not None:
                    dve.wait_ge(w_bias_sum, n + 1)
                    for k in range(KC):
                        ins = dve.tensor_scalar(staged(n)[:, k, :], staged(n)[:, k, :], ln[:, 0, k:k + 1], None, ALU.mult)
                    ins.then_inc(w_scaled, 1)
                    raw, dst, cols = ((bqkv_raw, qkv_bias, 6), (bfc_raw, fc_bias, FB))[n]
                    dve.tensor_tensor(dst[:], wide[n][:, 0:cols], raw[:], ALU.add).then_inc(w_bias, 1)
                    dve.wait_ge(w_scaled, n + 1)
                dve.wait_ge(w_hi, n + 1)
                dve.tensor_tensor(w[1][:], staged(n), w[0][:].bitcast(F32), ALU.subtract).then_inc(w_lo, 1)
            mask4 = bass.AP(mask[:].tensor, 0, [[P, P], [0, 4], [1, P]])

            def body(i, peeled):
                a, q, b, m, f, e = i, i - 1, i - 2, i - 3, i - 4, i - 5

                def masks(n):
                    used = (a_used, b, n - 3, 8) if n >= 4 else (a_used, b - 1, n + 5, 8)
                    after(dve, (scored, b, n + 1, 8), used)
                    dve.tensor_tensor(A[:, n % 4, :].rearrange("p (c r) -> p c r", c=4),
                                      score[n % 2][:, :].rearrange("p (c r) -> p c r", c=4), mask4, ALU.mult).then_inc(masked, 1)

                def lo_part(dst, hi, hi_sem, tile, readers, signal):
                    after(dve, (hi_sem, tile, 1, 1), *readers)
                    dve.tensor_tensor(dst[:, :, :].rearrange("p k t -> p (k t)"), turn[:, :],
                                      hi[:, :, :].rearrange("p k t -> p (k t)").bitcast(F32), ALU.subtract).then_inc(signal, 1)

                def hidden_lo(tile, n, hi_sem, signal):
                    after(dve, (hi_sem, tile, n + 1, 4))
                    dve.tensor_tensor(HB[1][:, 2 * n:2 * n + 2, :].rearrange("p k t -> p (k t)"), HF[:, n % 2, :],
                                      HB[0][:, 2 * n:2 * n + 2, :].rearrange("p k t -> p (k t)").bitcast(F32),
                                      ALU.subtract).then_inc(signal, 1)

                def statistics(n, src, tile, source_sem, per):
                    after(dve, (source_sem, tile, per, per), own=True)
                    for g in range(TA):
                        ins = dve.bn_stats(bn[n][:, g, :], src[:, g, :])
                    ins.then_inc(bn_done[n], 1)
                    after(dve, (bn_done[n], tile, 1, 1), own=True)
                    for g in range(TA):
                        ins = dve.bn_aggr(mv[n][:, g, :], bn[n][:, g, :])
                    ins.then_inc(stats[n], 1)

                def normalise(dst, src, n, r, signal):
                    for g in range(TA):
                        ins = dve.tensor_scalar(dst[:, g, :], src[:, g, :], mv[n][:, g, 0:1], r[:, g:g + 1],
                                                ALU.subtract, ALU.mult)
                    ins.then_inc(signal, 1)

                def work(*steps):
                    for kind, n in steps:
                        if kind == "mask" and live(b):
                            masks(n)
                        elif kind == "hidden" and live(m):
                            hidden_lo(m, n, h_hi, h_lo)

                work(("mask", 0))
                if live(m):
                    after(dve, (scale["x2"], m, 2, 2), (res_ready, m, 1, 1))
                    normalise(X2, X2, "x2", rs["x2"], z2_ready)
                work(("mask", 1))
                if live(e):
                    after(dve, (w2_ready, e, 1, 1), (x3b_ready, e, 1, 1), (stored, e - 1, 32, 32))
                    dve.tensor_tensor(OUTB[:].rearrange("p a c -> p (a c)"), rows[:, :], X3B[:].rearrange("p a c -> p (a c)"),
                                      ALU.add).then_inc(out_ready, 1)
                work(("mask", 2))
                if live(m):
                    lo_part(Z2T[1], Z2T[0], z2h, m, [(fc_ready, m - 1, 4, 4)], z2l)
                work(("mask", 3), ("mask", 4))
                if live(q):
                    lo_part(ZT[1], ZT[0], zh, q, [(vqk_ready, q - 1, 3, 3)], zl)
                if live(f):
                    after(dve, (scale["x3"], f, 2, 2), (z3_turned, f - 1, 1, 1))
                    normalise(Z3, X3, "x3", rs["x3"], z3_ready)
                work(("mask", 5), ("hidden", 0), ("mask", 6), ("hidden", 1), ("mask", 7), ("hidden", 2), ("hidden", 3))
                if live(b):
                    statistics("xc", XC, b, xc_loaded, 32)
                if live(f):
                    lo_part(Z3T[1], Z3T[0], z3h, f, [(w1_ready, f - 1, 4, 4)], z3l)

                def elu(t):
                    after(dve, (qk_act, q, t + 1, 2))
                    dve.scalar_tensor_tensor(EXPRELU[:, t, :], EXPRELU[:, t, :], 1.0, EXPRELU[:, 2 + t, :],
                                             ALU.min, ALU.add).then_inc(qk_made, 1)

                if live(a):
                    statistics("x", X, a, x_loaded, 16)
                if live(q):
                    elu(0)
                if live(b):
                    after(dve, (scale["xc"], b, 2, 2), (x2_ready, b - 1, 1, 1))
                    normalise(Y, XC, "xc", rs["xc"], y_ready)
                if live(q):
                    elu(1)
                if live(b):
                    after(dve, (den_moved, b, 64, 64))
                    dve.reciprocal(DD[:].rearrange("p j m t -> p (j m t)"), DD[:].rearrange("p j m t -> p (j m t)"))\
                       .then_inc(den_inverted, 1)
                    after(dve, (num_moved, b, 64, 64), (den_inverted, b, 1, 1), (at_hi, b - 1, 1, 1), (at_lo, b - 1, 1, 1))
                    for g in range(TA):
                        dve.tensor_tensor(AT[:, g, :, :].rearrange("p m (j t) -> p j m t", j=2), NN[:, 2 * g:2 * g + 2, :, :],
                                          DD[:, 2 * g:2 * g + 2, :, :], ALU.mult).then_inc(at_made, 1)
                if live(m):
                    after(dve, (proj_ready, m, 1, 1), (res_ready, m, 1, 1), (x3b_ready, m - 1, 1, 1), (z3_ready, m - 1, 1, 1))
                    dve.tensor_tensor(X3[:].rearrange("p a c -> p (a c)"), rows[:, :], RES[:].rearrange("p a c -> p (a c)"),
                                      ALU.add).then_inc(x3_ready, 1)
                if live(f):
                    hidden_lo(f, 0, g_hi, g_lo)
                if live(b):
                    after(dve, (at_hi, b, 1, 1), (o_ready, b - 1, 1, 1))
                    dve.tensor_tensor(ATL[:].rearrange("p g m t -> p (g m t)"), AT[:].rearrange("p g m t -> p (g m t)"),
                                      ATH[:].rearrange("p g m t -> p (g m t)").bitcast(F32), ALU.subtract).then_inc(at_lo, 1)

                def qk_low(t, moved):
                    after(dve, (qk_hi, q, t + 1, 2), (moved, q - 1, 96, 96))
                    dve.tensor_tensor(QKL[t][:, :, :].rearrange("p g n -> p (g n)"), EXPRELU[:, t, :],
                                      QKH[t][:, :, :].rearrange("p g n -> p (g n)").bitcast(F32),
                                      ALU.subtract).then_inc(qk_lo, 1)

                if live(q):
                    qk_low(0, q_moved)
                if live(f):
                    hidden_lo(f, 1, g_hi, g_lo)
                if live(q):
                    qk_low(1, k_moved)
                if live(b):
                    after(dve, (o_ready, b, 1, 1), (yb_ready, b, 1, 1), (z2_turned, b - 1, 1, 1))
                    dve.tensor_tensor(X2[:].rearrange("p a c -> p (a c)"), rows[:, :], Y[:].rearrange("p a c -> p (a c)"),
                                      ALU.add).then_inc(x2_ready, 1)
                if live(f):
                    hidden_lo(f, 2, g_hi, g_lo)
                if live(f):
                    hidden_lo(f, 3, g_hi, g_lo)
                if live(b):
                    statistics("x2", X2, b, x2_ready, 1)
                if live(m):
                    statistics("x3", X3, m, x3_ready, 1)
                if live(a):
                    after(dve, (scale["x"], a, 7, 7))
                    normalise(X, X, "x", rz, z_ready)

            run(dve, body)


def kernel(**inputs):
    import numpy as np
    import concourse.bacc as bacc
    from concourse.bass_utils import run_bass_kernel_spmd

    def channels(w, axis):
        w = np.moveaxis(np.asarray(w), axis, 0)
        w = w.reshape((H // 2, 2, D) + w.shape[1:])
        w = np.moveaxis(w, 0, 2).reshape((C,) + w.shape[3:])
        return np.ascontiguousarray(np.moveaxis(w, 0, axis))

    def columns(v):
        return np.ascontiguousarray(np.asarray(v).reshape(-1, P).T)

    g = lambda name: np.asarray(inputs["L0_" + name])
    qkv = ("q", "k", "v")
    r = np.arange(P)
    arrays = {
        "x": np.ascontiguousarray(g("attn_x").reshape(T, C)),
        "wqkv": np.ascontiguousarray(np.concatenate([channels(g(f"attn_{n}_w"), 0).T for n in qkv], axis=1)),
        "bqkv": np.ascontiguousarray(np.concatenate([columns(channels(g(f"attn_{n}_b"), 0)) for n in qkv], axis=1)),
        "ln1w": columns(g("attn_ln1_w")), "ln1b": columns(g("attn_ln1_b")),
        "wo": np.ascontiguousarray(channels(g("attn_o_w"), 1).T), "bo": g("attn_o_b"),
        "ln2w": columns(g("attn_ln2_w")), "ln2b": columns(g("attn_ln2_b")),
        "wfc": np.ascontiguousarray(g("attn_fc_w").T), "bfc": columns(g("attn_fc_b")),
        "wproj": np.ascontiguousarray(g("attn_proj_w").T), "bproj": g("attn_proj_b"),
        "w1": np.ascontiguousarray(g("ffn_W1")), "b1": columns(g("ffn_b1")),
        "w2": np.ascontiguousarray(g("ffn_W2")), "b2": g("ffn_b2"),
        "ident": np.eye(P, dtype=np.float32),
        "mask": (r[:, None] % CH == r[None, :] % CH).astype(np.float32),
    }
    nc = bacc.Bacc("TRN2", target_bir_lowering=False, num_devices=1)
    args = [nc.dram_tensor(f"in_{name}", a.shape, mybir.dt.from_np(a.dtype), kind="ExternalInput").ap() for name, a in arrays.items()]
    result = nc.dram_tensor("result", (T, C), F32, kind="ExternalOutput").ap()
    build(nc, *args, result)
    got = run_bass_kernel_spmd(nc, [{f"in_{n}": a for n, a in arrays.items()}], core_ids=[0])
    return got.results[0]["result"].reshape(8, T // 8, C)
```

```python
from contextlib import ExitStack

import concourse.bass as bass
from concourse import mybir

F32 = mybir.dt.float32
F32R = mybir.dt.float32r
ALU = mybir.AluOpType
ACT = mybir.ActivationFunctionType

P = 128
T = 8192
C = 256
KC = C // P
F = 1024
FB = F // P
H, D = 16, 16
TT = 256
TA = TT // P
NT = T // TT
CH = P // H
NCH = P // CH
EPS = 1e-5
DEPTH = 5


def after(eng, *needs, own=False):
    values = []
    for sem, tile, k, per in needs:
        if isinstance(tile, int):
            if tile >= 0:
                values.append((sem, min(tile, NT - 1) * per + (k if tile < NT else per)))
        else:
            values.append((sem, eng.snap(tile * per + k)))
    for sem, value in values:
        eng.wait_ge(sem, value)
        if own and not isinstance(value, int):
            eng.nop(nofuse=True)


def live(tile):
    return not isinstance(tile, int) or 0 <= tile < NT


def run(eng, body):
    for i in range(DEPTH + 1):
        body(i, True)
    with eng.Fori(DEPTH + 1, NT) as i:
        body(i, False)
    for i in range(NT, NT + DEPTH):
        body(i, True)


def build(nc, x, wqkv, bqkv, ln1w, ln1b, wo, bo, ln2w, ln2b, wfc, bfc, wproj, bproj, w1, b1, w2, b2, ident_in, mask_in, out):
    with ExitStack() as ctx:
        def sb(name, shape, dt=F32):
            return ctx.enter_context(nc.sbuf_tensor(name, shape, dt))

        def sem(name):
            return ctx.enter_context(nc.semaphore(name))

        WQKV = [sb(f"wqkv_{p}", [P, KC, 3 * C], F32R) for p in "hl"]
        WO = [sb(f"wo_{p}", [P, KC, C], F32R) for p in "hl"]
        WFC = [sb(f"wfc_{p}", [P, KC, F], F32R) for p in "hl"]
        WPROJ = [sb(f"wproj_{p}", [P, FB, C], F32R) for p in "hl"]
        W1 = [sb(f"w1_{p}", [P, KC, F], F32R) for p in "hl"]
        W2 = [sb(f"w2_{p}", [P, FB, C], F32R) for p in "hl"]
        ident = sb("ident", [P, P])
        mask = sb("mask", [P, P])
        bqkv_raw = sb("bqkv_raw", [P, 6])
        bfc_raw = sb("bfc_raw", [P, FB])
        qkv_bias = sb("qkv_bias", [P, 6])
        fc_bias = sb("fc_bias", [P, FB])
        b1_sb = sb("b1_sb", [P, FB])
        ln1 = sb("ln1", [P, 2, KC])
        ln2 = sb("ln2", [P, 2, KC])
        bo_rows = sb("bo_rows", [P, C])
        bproj_rows = sb("bproj_rows", [P, C])
        b2_rows = sb("b2_rows", [P, C])
        minus_half = sb("minus_half", [P, TA])
        X = sb("X", [P, TA, C])
        XC = sb("XC", [P, TA, C])
        early = sb("early_rows", [P, 4, TA * C])
        late = sb("late_rows", [P, 4, TA * C])
        Y, X2, RES = (early[:, n, :].rearrange("p (a c) -> p a c", a=TA) for n in range(3))
        X3, Z3, X3B, OUTB = (late[:, n, :].rearrange("p (a c) -> p a c", a=TA) for n in range(4))
        ZT = [sb(f"zt_{p}", [P, KC, TT], F32R) for p in "hl"]
        Z2T = [sb(f"z2t_{p}", [P, KC, TT], F32R) for p in "hl"]
        Z3T = [sb(f"z3t_{p}", [P, KC, TT], F32R) for p in "hl"]
        HB = [sb(f"hidden_{p}", [P, FB, TT], F32R) for p in "hl"]
        HF = sb("hidden_f32", [P, 2, 2 * TT])
        EXPRELU = sb("exp_relu", [P, 4, TA * KC * P])
        QKH = [sb(f"{n}_hi", [P, TA, KC * P], F32R) for n in "qk"]
        QKL = [sb(f"{n}_lo", [P, TA, KC * P], F32R) for n in "qk"]
        VN = sb("VN", [P, TA, KC * P])
        QD = sb("QD", [P, H * P], F32R)
        KD = sb("KD", [P, H * P], F32R)
        VD = sb("VD", [P, H * P])
        VC = sb("VC", [P, TA * NCH, 2 * D])
        A = sb("A", [P, 4, 4 * P])
        ND = sb("ND", [P, H, 8, 8])
        NN = sb("NN", [P, 4, 2, 64])
        DD = sb("DD", [P, 4, 2, 64])
        AT = early[:, 3, :].rearrange("p (g m t) -> p g m t", g=TA, m=KC)
        ATH = sb("AT_hi", [P, TA, KC, P], F32R)
        ATL = sb("AT_lo", [P, TA, KC, P], F32R)
        bn = {n: sb(f"bn_{n}", [P, TA, 6]) for n in ("x", "xc", "x2", "x3")}
        mv = {n: sb(f"mv_{n}", [P, TA, 2]) for n in ("x", "xc", "x2", "x3")}
        ve = {n: sb(f"ve_{n}", [P, TA]) for n in ("x", "xc", "x2", "x3")}
        rs = {n: sb(f"rs_{n}", [P, TA]) for n in ("x", "xc", "x2", "x3")}
        sq = sb("sq", [P, TA])
        sv = sb("sv", [P, TA])
        se = sb("se", [P, TA])
        rz1 = sb("rz1", [P, TA])
        rz = sb("rz", [P, TA])

        def bank(name):
            return ctx.enter_context(nc.psum_tensor(name, [P, 512], F32))
        turn = bank("turn")
        wide = [bank("wide_a"), bank("wide_b")]
        rows = bank("rows")
        score = [bank("score_0"), bank("score_1")]
        summed = [bank("summed_0"), bank("summed_1")]

        first_loaded, others_loaded = sem("first_loaded"), sem("others_loaded")
        w_loaded = [sem(f"w_loaded_{n}") for n in range(7)]
        w_scaled, w_hi, w_lo, w_bias_sum, w_bias = (sem(n) for n in ("w_scaled", "w_hi", "w_lo", "w_bias_sum", "w_bias"))
        ones_set = sem("ones_set")
        x_loaded = sem("x_loaded")
        xc_loaded = sem("xc_loaded")
        bn_done = {n: sem(f"bn_done_{n}") for n in bn}
        stats = {n: sem(f"stats_{n}") for n in bn}
        scale = {n: sem(f"scale_{n}") for n in bn}
        z_ready, z2_ready, z3_ready = sem("z_ready"), sem("z2_ready"), sem("z3_ready")
        z_turned, z2_turned, z3_turned = sem("z_turned"), sem("z2_turned"), sem("z3_turned")
        zh, z2h, z3h = sem("zh"), sem("z2h"), sem("z3h")
        zl, z2l, z3l = sem("zl"), sem("z2l"), sem("z3l")
        vqk_ready = sem("vqk_ready")
        qk_act = sem("qk_act")
        v_act = sem("v_act")
        qk_made = sem("qk_made")
        qk_hi = sem("qk_hi")
        qk_lo = sem("qk_lo")
        q_moved, k_moved = sem("q_moved"), sem("k_moved")
        v_moved = sem("v_moved")
        v_turned = sem("v_turned")
        vc_ready = sem("vc_ready")
        scored = sem("scored")
        masked = sem("masked")
        a_used = sem("a_used")
        nd_ready = sem("nd_ready")
        num_moved, den_moved = sem("num_moved"), sem("den_moved")
        den_inverted = sem("den_inverted")
        at_made = sem("at_made")
        at_hi, at_lo = sem("at_hi"), sem("at_lo")
        y_ready, yb_ready = sem("y_ready"), sem("yb_ready")
        xc_biased = sem("xc_biased")
        o_ready, x2_ready, res_ready = sem("o_ready"), sem("x2_ready"), sem("res_ready")
        fc_ready, gelu_made, h_hi, h_lo = sem("fc_ready"), sem("gelu_made"), sem("h_hi"), sem("h_lo")
        proj_ready, x3_ready, x3b_ready = sem("proj_ready"), sem("x3_ready"), sem("x3b_ready")
        w1_ready, relu_made, g_hi, g_lo = sem("w1_ready"), sem("relu_made"), sem("g_hi"), sem("g_lo")
        w2_ready, out_ready = sem("w2_ready"), sem("out_ready")
        stored = sem("stored")

        x_rows = x.rearrange("(n p a) c -> n p (a c)", p=P, a=TA)
        x_rows_c = x.rearrange("(n s jj i a) c -> n jj s i (a c)", s=8, jj=2, i=8, a=TA)
        out_rows_c = out.rearrange("(n s jj i a) c -> n jj s i (a c)", s=8, jj=2, i=8, a=TA)

        def flat(tile):
            return tile[:].rearrange({3: "p a b -> p (a b)", 4: "p a b c -> p (a b c)"}[len(tile.shape)])

        half = [FB // 2 * m for m in range(3)]
        rows_of = lambda w, a, b: w[P * a:P * b, :].rearrange("(k p) n -> p k n", p=P)
        WEIGHTS = [
            (rows_of(wqkv, 0, KC), [w[:] for w in WQKV], ln1, VD[:, :]),
            (rows_of(wfc, 0, KC), [w[:] for w in WFC], ln2, flat(A)),
            (rows_of(wo, 0, KC), [w[:] for w in WO], None, flat(NN)),
            (rows_of(wproj, 0, FB), [w[:] for w in WPROJ], None, flat(late)),
            (rows_of(w1, 0, KC), [w[:] for w in W1], None, flat(early)),
            (rows_of(w2, half[0], half[1]), [w[:, half[0]:half[1], :] for w in W2], None, flat(HF)),
            (rows_of(w2, half[1], half[2]), [w[:, half[1]:half[2], :] for w in W2], None, flat(ND)),
        ]
        BIASES = [(summed[0], bqkv_raw, qkv_bias, 6), (rows, bfc_raw, fc_bias, FB)]

        def staged(n):
            _, blocks, width = WEIGHTS[n][0].shape
            return WEIGHTS[n][3][:, 0:blocks * width].rearrange("p (k n) -> p k n", k=blocks)

        IN_FRONT = {1: (0,), 2: (2, 3, 4, 5, 6)}
        IN_MIDDLE = {1: (1,)}

        block = ctx.enter_context(nc.Block())

        @block.sync
        def _(sp):
            first = [(ident[:], ident_in), (ln1[:, 0, :], ln1w), (ln1[:, 1, :], ln1b), (bqkv_raw[:], bqkv)]
            others = [(mask[:], mask_in), (ln2[:, 0, :], ln2w), (ln2[:, 1, :], ln2b), (bfc_raw[:], bfc), (b1_sb[:], b1),
                      (bo_rows[:], bo.partition_broadcast(P)), (bproj_rows[:], bproj.partition_broadcast(P)),
                      (b2_rows[:], b2.partition_broadcast(P))]

            def load_weight(n):
                sp.dma_start(staged(n), WEIGHTS[n][0]).then_inc(w_loaded[n], 16)

            sp.dma_start(X[:, :, :].rearrange("p a c -> p (a c)"), x_rows[0]).then_inc(x_loaded, 16)
            for dst, src in first:
                sp.dma_start(dst, src).then_inc(first_loaded, 16)
            load_weight(0)
            load_weight(1)
            for dst, src in others:
                sp.dma_start(dst, src).then_inc(others_loaded, 16)
            for n in range(2, len(WEIGHTS)):
                load_weight(n)

            def body(i, peeled):
                a, q, c, e = i, i - 1, i - 2, i - 5
                if live(c):
                    after(sp, (res_ready, c - 1, 1, 1), own=True)
                    for jj in range(2):
                        sp.dma_start(XC[64 * jj:64 * jj + 64, :, :].rearrange("p a c -> p (a c)"),
                                     x_rows_c[c, jj]).then_inc(xc_loaded, 16)
                if live(a) and not (isinstance(i, int) and i == 0):
                    after(sp, (z_turned, a - 1, 1, 1), own=True)
                    sp.dma_start(X[:, :, :].rearrange("p a c -> p (a c)"), x_rows[a]).then_inc(x_loaded, 16)
                if live(e):
                    after(sp, (out_ready, e, 1, 1), own=True)
                    for jj in range(2):
                        sp.dma_start(out_rows_c[e, jj],
                                     OUTB[64 * jj:64 * jj + 64, :, :].rearrange("p a c -> p (a c)")).then_inc(stored, 16)
                if live(c):
                    after(sp, (nd_ready, c, 2, 2), (at_made, c - 1, 2, 2), own=True)
                    for dst, part, moved in ((DD, D, den_moved), (NN, 0, num_moved)):
                        for j in range(4):
                            sp.dma_start(dst[:, j, :, :].rearrange("p m t -> p (m t)"),
                                         ND[32 * j + part:32 * j + part + D, :, :, :].rearrange("p h s i -> p (h s i)"))\
                              .then_inc(moved, 16)
                if live(q):
                    after(sp, (v_act, q, 1, 1), (v_turned, q - 1, 1, 1), own=True)
                    for g in range(TA):
                        sp.dma_start(VD[D * g:D * g + D, :], VN[:, g, :]).then_inc(v_moved, 16)
                    after(sp, (scored, q - 1, 8, 8), own=True)
                    for t, (dst, his, moved) in enumerate(((QD, (0, 2), q_moved), (KD, (0, 1), k_moved))):
                        after(sp, (qk_hi, q, t + 1, 2), own=True)
                        for g in range(TA):
                            for h in his:
                                sp.dma_start(dst[64 * g + D * h:64 * g + D * h + D, :].bitcast(F32),
                                             QKH[t][:, g, :].bitcast(F32)).then_inc(moved, 16)
                    for t, (dst, lo, moved) in enumerate(((QD, 1, q_moved), (KD, 2, k_moved))):
                        after(sp, (qk_lo, q, t + 1, 2), own=True)
                        for g in range(TA):
                            sp.dma_start(dst[64 * g + D * lo:64 * g + D * lo + D, :].bitcast(F32),
                                         QKL[t][:, g, :].bitcast(F32)).then_inc(moved, 16)

            run(sp, body)
            sp.wait_ge(stored, 32 * NT)

        @block.tensor
        def _(pe):
            pe.wait_ge(first_loaded, 16 * 4)

            def shift_sums(n):
                _, _, ln, _ = WEIGHTS[n]
                bank, _, _, blocks = BIASES[n]
                pe.wait_ge(w_loaded[n], 16)
                for m in range(blocks):
                    for k in range(KC):
                        mm = pe.matmul(bank[:, m:m + 1], staged(n)[:, k, P * m:P * m + P], ln[:, 1, k:k + 1],
                                       start=(k == 0), stop=(k == KC - 1))
                mm.then_inc(w_bias_sum, 1)

            def product(dst, hi_lo_w, hi_lo_x, parts, last_sem=None):
                passes = [(0, 0), (1, 0), (0, 1)]
                n = len(parts)
                for k, (w, xx) in enumerate(parts):
                    for m, (pw, px) in enumerate(passes):
                        mm = pe.matmul(dst, w(hi_lo_w[pw]), xx(hi_lo_x[px]), start=(k == 0 and m == 0),
                                       stop=(k == n - 1 and m == 2))
                return mm

            def turn_rows(z):
                for g in range(TA):
                    for k in range(KC):
                        mm = pe.transpose(turn[:, TT * k + P * g:TT * k + P * g + P], z[:, g, P * k:P * k + P], ident[:])
                return mm

            def blocks_of(w, zt, first, dst):
                for b in range(2):
                    lo = P * (first + b)
                    mm = product(dst[:, TT * b:TT * b + TT], w, zt,
                                 [(lambda v, k=k: v[:, k, lo:lo + P], lambda v, k=k: v[:, k, :]) for k in range(KC)])
                return mm

            def token_rows(act, w, count, in_front=None, groups=range(TA)):
                for g in groups:
                    dst = rows[:, C * g:C * g + C]
                    for k in range(count):
                        if in_front:
                            in_front(g, k)
                        for m, (pa, pw) in enumerate([(0, 0), (1, 0), (0, 1)]):
                            mm = pe.matmul(dst, act(pa, k, g), w[pw][:, k, :], start=(k == 0 and m == 0),
                                           stop=(k == count - 1 and m == 2))
                return mm

            def chunks(n):
                g, k = n % 2, n // 2
                for c, i in enumerate((2 * k, 2 * k + 1, 8 + 2 * k, 8 + 2 * k + 1)):
                    yield g, c, i, 2 * g + i // 8, i % 4

            def body(i, peeled):
                q, b, m, f, e = i - 1, i - 2, i - 3, i - 4, i - 5
                if peeled and i == 1:
                    shift_sums(0)

                def scores(n):
                    if n == 0:
                        after(pe, (q_moved, b, 96, 96), (k_moved, b, 96, 96), (masked, b - 1, 7, 8))
                    elif n == 1:
                        after(pe, (masked, b - 1, 8, 8))
                    else:
                        after(pe, (masked, b, n - 1, 8))
                    for g, c, ch, _, _ in chunks(n):
                        mm = pe.matmul(score[g][:, P * c:P * c + P], KD[64 * g:64 * g + 3 * D, ch:H * P:NCH],
                                       QD[64 * g:64 * g + 3 * D, ch:H * P:NCH], start=True, stop=True)
                    mm.then_inc(scored, 1)

                def weighted(n):
                    if n == 0:
                        after(pe, (vc_ready, b, 1, 1), (masked, b, 1, 8), (nd_ready, b - 1, 1, 2))
                    elif n == 4:
                        after(pe, (masked, b, 5, 8), (nd_ready, b - 1, 2, 2))
                    else:
                        after(pe, (masked, b, n + 1, 8))
                    for g, c, ch, j, place in chunks(n):
                        mm = pe.matmul(summed[n // 4][32 * j:32 * j + 32, P * place:P * place + P], VC[:, NCH * g + ch, :],
                                       A[:, n % 4, P * c:P * c + P], start=True, stop=True)
                    mm.then_inc(a_used, 1)

                def turn_z2():
                    extra = [(z3l, f - 1, 1, 1)] if peeled else []
                    after(pe, (z2_ready, m, 1, 1), (vc_ready, b, 1, 1), *extra)
                    turn_rows(X2).then_inc(z2_turned, 1)

                def attend(*steps):
                    if live(b):
                        for n in steps:
                            weighted(n)
                            if n + 2 < 8:
                                scores(n + 2)

                for g in range(TA):
                    if live(e):
                        if g == 0:
                            extra = [(x3_ready, m - 1, 1, 1), (out_ready, e - 1, 1, 1)] if peeled else []
                            after(pe, (x2_ready, b - 1, 1, 1), *extra)

                        if peeled:
                            pe.wait_ge(w_lo, 7)

                        def in_front(g, k):
                            if g == 0 and k % 2 == 0:
                                after(pe, (g_lo, e, k // 2 + 1, 4))
                            elif g == 1 and k == FB // 2 and live(m):
                                turn_z2()
                        mm = token_rows(lambda part, k, g: HB[part][:, k, P * g:P * g + P], W2, FB, in_front, [g])
                        if g == TA - 1:
                            mm.then_inc(w2_ready, 1)
                    if g == 0 and live(b):
                        scores(0)
                        scores(1)
                if live(m) and not live(e):
                    turn_z2()
                attend(0, 1)
                if live(q):
                    extra = [(vc_ready, q - 1, 1, 1)] if peeled else []
                    after(pe, (z_ready, q, 1, 1), (z2l, m, 1, 1), *extra)
                    turn_rows(X).then_inc(z_turned, 1)
                if peeled and i == 1:
                    pe.wait_ge(others_loaded, 16 * 8)
                    shift_sums(1)
                attend(2)
                for n, steps in enumerate(((3,), (4,), (5, 6), (7,))):
                    if live(m):
                        if n == 0:
                            extra = [(qk_act, q - 1, 2, 2), (gelu_made, m - 1, 4, 4)] if peeled else []
                            after(pe, (z2l, m, 1, 1), (relu_made, f - 1, 4, 4), *extra)
                        elif n >= 2:
                            after(pe, (gelu_made, m, n - 1, 4))
                        if peeled:
                            pe.wait_ge(w_lo, 2)
                        blocks_of(WFC, Z2T, 2 * n, wide[n % 2]).then_inc(fc_ready, 1)
                    attend(*steps)
                if live(f):
                    extra = [(z2l, m, 1, 1), (z3l, f - 1, 1, 1)] if peeled else []
                    after(pe, (z3_ready, f, 1, 1), (zl, q, 1, 1), *extra)
                    turn_rows(Z3).then_inc(z3_turned, 1)
                if live(q):
                    for n, t in enumerate((2, 0, 1)):
                        if n == 0:
                            extra = [(qk_act, q - 1, 2, 2)] if peeled else []
                            after(pe, (zl, q, 1, 1), (gelu_made, m, 3, 4), *extra)
                        elif n == 1:
                            after(pe, (gelu_made, m, 4, 4))
                        else:
                            after(pe, (v_act, q, 1, 1))
                        if peeled:
                            pe.wait_ge(w_lo, 1)
                        blocks_of(WQKV, ZT, 2 * t, wide[n % 2]).then_inc(vqk_ready, 1)
                if live(m):
                    extra = [(x2_ready, b - 1, 1, 1)] if peeled else []
                    after(pe, (out_ready, e, 1, 1), *extra)

                    def h_block(g, k):
                        if g == 0 and k % 2 == 0:
                            after(pe, (h_lo, m, k // 2 + 1, 4))
                    if peeled:
                        pe.wait_ge(w_lo, 4)
                    token_rows(lambda part, k, g: HB[part][:, k, P * g:P * g + P], WPROJ, FB, h_block).then_inc(proj_ready, 1)
                def output_projection():
                    if not live(b):
                        return
                    after(pe, (at_hi, b, 1, 1), (at_lo, b, 1, 1), (x3_ready, m, 1, 1))
                    if peeled:
                        pe.wait_ge(w_lo, 3)
                    token_rows(lambda part, k, g: (ATH, ATL)[part][:, g, k, :], WO, KC).then_inc(o_ready, 1)
                if live(f):
                    for n in range(4):
                        if n == 3:
                            output_projection()
                        if n == 0:
                            extra = [(gelu_made, m, 4, 4), (relu_made, f - 1, 4, 4)] if peeled else []
                            after(pe, (z3l, f, 1, 1), (qk_act, q, 1, 2), *extra)
                        elif n == 1:
                            after(pe, (qk_act, q, 2, 2))
                        else:
                            after(pe, (relu_made, f, n - 1, 4))
                        if peeled:
                            pe.wait_ge(w_lo, 5)
                        blocks_of(W1, Z3T, 2 * n, wide[(n + 1) % 2]).then_inc(w1_ready, 1)
                if not live(f):
                    output_projection()
                if live(q):
                    extra = [(zl, q, 1, 1)] if peeled else []
                    after(pe, (v_moved, q, 32, 32), (z3l, f, 1, 1), *extra, own=True)
                    for ch in range(NCH):
                        mm = pe.transpose(turn[:, TA * D * ch:TA * D * ch + TA * D], VD[0:TA * D, ch:H * P:NCH],
                                          ident[0:TA * D, 0:TA * D])
                    mm.then_inc(v_turned, 1)

            run(pe, body)

        @block.scalar
        def _(act):
            def prepare(weights):
                for n in weights:
                    _, w, ln, _ = WEIGHTS[n]
                    act.wait_ge(w_loaded[n], 16)
                    if ln is not None:
                        act.wait_ge(w_scaled, n + 1)
                    act.activation(w[0], staged(n), ACT.Copy).then_inc(w_hi, 1)
                    if ln is not None:
                        act.wait_ge(w_bias, n + 1)
                    else:
                        act.wait_ge(others_loaded, 16 * 8)

            def body(i, peeled):
                q, b, m, f = i - 1, i - 2, i - 3, i - 4
                if peeled:
                    prepare(IN_FRONT.get(i, ()))

                def sums(u):
                    after(act, (a_used, b, 4 * u + 4, 8), *([(num_moved, b - 1, 64, 64), (den_moved, b - 1, 64, 64)] if u == 0 else []))
                    act.activation(ND[:, :, :, 4 * u:4 * u + 4].rearrange("p h s i -> p i h s"),
                                   summed[u][:, :].rearrange("p (i h s) -> p i h s", i=4, h=H), ACT.Copy).then_inc(nd_ready, 1)

                def hi_part(dst, turned, tile, readers, signal):
                    after(act, (turned, tile, 1, 1), *readers)
                    act.activation(dst[:, :, :].rearrange("p k t -> p (k t)"), turn[:, :], ACT.Copy).then_inc(signal, 1)

                def hidden_hi(tile, n, made, readers, signal):
                    after(act, (made, tile, n + 1, 4), *(readers if n == 0 else []))
                    act.activation(HB[0][:, 2 * n:2 * n + 2, :].rearrange("p k t -> p (k t)"), HF[:, n % 2, :],
                                   ACT.Copy).then_inc(signal, 1)

                if live(m):
                    hi_part(Z2T[0], z2_turned, m, [(fc_ready, m - 1, 4, 4)], z2h)
                if live(q):
                    hi_part(ZT[0], z_turned, q, [(vqk_ready, q - 1, 3, 3)], zh)
                if peeled:
                    prepare(IN_MIDDLE.get(i, ()))
                for n in range(4):
                    if live(m):
                        extra = [(h_lo, m - 1, 4, 4)] if peeled and n < 2 else []
                        free = (g_lo, f - 1, 4, 4) if n < 2 else (h_lo, m, n - 1, 4)
                        after(act, (fc_ready, m, n + 1, 4), free, *extra)
                        for k in range(2):
                            ins = act.activation(HF[:, n % 2, TT * k:TT * k + TT], wide[n % 2][:, TT * k:TT * k + TT], ACT.Gelu,
                                                 bias=fc_bias[:, 2 * n + k:2 * n + k + 1])
                        ins.then_inc(gelu_made, 1)
                        extra = [(proj_ready, m - 1, 1, 1)] if peeled else []
                        hidden_hi(m, n, gelu_made, [(w2_ready, f - 1, 1, 1), *extra], h_hi)
                    if live(b) and n in (2, 3):
                        sums(n - 2)
                if live(q):
                    after(act, (vqk_ready, q, 1, 3), (v_moved, q - 1, 32, 32))
                    for k in range(KC):
                        ins = act.activation(VN[:, :, :].rearrange("p g (m t) -> p g m t", m=KC)[:, :, k, :],
                                             wide[0][:, TT * k:TT * k + TT].rearrange("p (g t) -> p g t", g=TA), ACT.Identity,
                                             bias=qkv_bias[:, 4 + k:5 + k])
                    ins.then_inc(v_act, 1)
                if live(f):
                    hi_part(Z3T[0], z3_turned, f, [(w1_ready, f - 1, 4, 4)], z3h)
                if live(q):
                    for t in range(2):
                        after(act, (vqk_ready, q, t + 2, 3), (qk_lo, q - 1, t + 1, 2))
                        for s, fn in ((0, ACT.Exp), (2, ACT.Relu)):
                            for k in range(KC):
                                ins = act.activation(
                                    EXPRELU[:, t + s, :].rearrange("p (g m t) -> p g m t", g=TA, m=KC)[:, :, k, :],
                                    wide[(t + 1) % 2][:, TT * k:TT * k + TT].rearrange("p (g t) -> p g t", g=TA), fn,
                                    bias=qkv_bias[:, 2 * t + k:2 * t + k + 1])
                        ins.then_inc(qk_act, 1)
                    for t, moved in enumerate((q_moved, k_moved)):
                        after(act, (qk_made, q, t + 1, 2), (moved, q - 1, 96, 96))
                        act.activation(QKH[t][:, :, :].rearrange("p g n -> p (g n)"), EXPRELU[:, t, :], ACT.Copy).then_inc(qk_hi, 1)
                for n in range(4):
                    if live(f):
                        extra = [(g_lo, f - 1, 4, 4)] if peeled and n < 2 else []
                        free = (h_lo, m, n + 3, 4) if n < 2 else (g_lo, f, n - 1, 4)
                        after(act, (w1_ready, f, n + 1, 4), free, *extra)
                        for k in range(2):
                            ins = act.activation(HF[:, n % 2, TT * k:TT * k + TT], wide[(n + 1) % 2][:, TT * k:TT * k + TT], ACT.Relu,
                                                 bias=b1_sb[:, 2 * n + k:2 * n + k + 1])
                        ins.then_inc(relu_made, 1)
                    if live(b) and n == 0:
                        after(act, (at_made, b, 2, 2), (o_ready, b - 1, 1, 1))
                        act.activation(ATH[:, :, :, :].rearrange("p g m t -> p (g m t)"),
                                       AT[:, :, :, :].rearrange("p g m t -> p (g m t)"), ACT.Copy).then_inc(at_hi, 1)
                    if live(f):
                        extra = [(w2_ready, f - 1, 1, 1)] if peeled else []
                        hidden_hi(f, n, relu_made, [(proj_ready, m, 1, 1), *extra], g_hi)
                if live(q):
                    after(act, (v_turned, q, 1, 1), (a_used, q - 1, 8, 8))
                    act.activation(VC[:, :, 0:D].rearrange("p (g c) e -> p c g e", g=TA),
                                   turn[:, :].rearrange("p (c g e) -> p c g e", g=TA, e=D), ACT.Copy).then_inc(vc_ready, 1)

            run(act, body)

        @block.gpsimd
        def _(pool):
            pool.memset(minus_half[:], -0.5).then_inc(ones_set, 1)
            pool.memset(VC[:, :, D:2 * D], 1.0).then_inc(ones_set, 1)
            pool.wait_ge(ones_set, 2)

            def body(i, peeled):
                a, b, m, f = i, i - 2, i - 3, i - 4
                if peeled and i == 2:
                    pool.wait_ge(others_loaded, 16 * 8)

                def inverse_root(n, tile, per):
                    after(pool, (stats[n], tile, 1, 1), own=True)
                    pool.tensor_scalar(ve[n][:], mv[n][:, :, 1], EPS, None, ALU.add).then_inc(scale[n], 1)
                    after(pool, (scale[n], tile, 1, per), own=True)
                    pool.tensor_tensor(rs[n][:], ve[n][:], minus_half[:], ALU.pow).then_inc(scale[n], 1)

                if live(b):
                    inverse_root("xc", b, 2)
                if live(a):
                    inverse_root("x", a, 7)
                    after(pool, (scale["x"], a, 2, 7), own=True)
                    pool.tensor_tensor(sq[:], rs["x"][:], rs["x"][:], ALU.mult).then_inc(scale["x"], 1)
                    after(pool, (scale["x"], a, 3, 7), own=True)
                    pool.tensor_tensor(sv[:], sq[:], mv["x"][:, :, 1], ALU.mult).then_inc(scale["x"], 1)
                    after(pool, (scale["x"], a, 4, 7), own=True)
                    pool.tensor_scalar(se[:], sv[:], EPS, None, ALU.add).then_inc(scale["x"], 1)
                    after(pool, (scale["x"], a, 5, 7), own=True)
                    pool.tensor_tensor(rz1[:], se[:], minus_half[:], ALU.pow).then_inc(scale["x"], 1)
                    after(pool, (scale["x"], a, 6, 7), own=True)
                    pool.tensor_tensor(rz[:], rz1[:], rs["x"][:], ALU.mult).then_inc(scale["x"], 1)
                if live(b):
                    after(pool, (y_ready, b, 1, 1), own=True)
                    for g in range(TA):
                        ins = pool.tensor_tensor(Y[:, g, :], Y[:, g, :], bo_rows[:], ALU.add)
                    ins.then_inc(yb_ready, 1)
                    for g in range(TA):
                        ins = pool.tensor_tensor(XC[:, g, :], XC[:, g, :], bproj_rows[:], ALU.add)
                    ins.then_inc(xc_biased, 1)
                if live(b):
                    inverse_root("x2", b, 2)
                    after(pool, (x2_ready, b, 1, 1), (xc_biased, b, 1, 1), (x3_ready, m, 1, 1), own=True)
                    pool.tensor_tensor(RES[:].rearrange("p a c -> p (a c)"), X2[:].rearrange("p a c -> p (a c)"),
                                       XC[:].rearrange("p a c -> p (a c)"), ALU.add).then_inc(res_ready, 1)
                if live(m):
                    inverse_root("x3", m, 2)
                if live(m):
                    after(pool, (x3_ready, m, 1, 1), (out_ready, f, 1, 1), own=True)
                    for g in range(TA):
                        ins = pool.tensor_tensor(X3B[:, g, :], X3[:, g, :], b2_rows[:], ALU.add)
                    ins.then_inc(x3b_ready, 1)

            run(pool, body)

        @block.vector
        def _(dve):
            def prepare(weights):
                for n in weights:
                    _, w, ln, _ = WEIGHTS[n]
                    dve.wait_ge(w_loaded[n], 16)
                    if ln is not None:
                        dve.wait_ge(first_loaded, 16 * 4)
                        if n > 0:
                            dve.wait_ge(others_loaded, 16 * 8)
                        dve.wait_ge(w_bias_sum, n + 1)
                        for k in range(KC):
                            ins = dve.tensor_scalar(staged(n)[:, k, :], staged(n)[:, k, :], ln[:, 0, k:k + 1], None, ALU.mult)
                        ins.then_inc(w_scaled, 1)
                        bank, raw, dst, blocks = BIASES[n]
                        dve.tensor_tensor(dst[:], bank[:, 0:blocks], raw[:], ALU.add).then_inc(w_bias, 1)
                        dve.wait_ge(w_scaled, n + 1)
                    dve.wait_ge(w_hi, n + 1)
                    dve.tensor_tensor(w[1], staged(n), w[0].bitcast(F32), ALU.subtract).then_inc(w_lo, 1)
                    dve.wait_ge(w_lo, n + 1)

            mask4 = bass.AP(mask[:].tensor, 0, [[P, P], [0, 4], [1, P]])

            def body(i, peeled):
                a, q, b, m, f, e = i, i - 1, i - 2, i - 3, i - 4, i - 5
                if peeled:
                    prepare(IN_FRONT.get(i, ()))

                def masks(n):
                    used = (a_used, b, n - 3, 8) if n >= 4 else (a_used, b - 1, n + 5, 8)
                    after(dve, (scored, b, n + 1, 8), used)
                    dve.tensor_tensor(A[:, n % 4, :].rearrange("p (c r) -> p c r", c=4),
                                      score[n % 2][:, :].rearrange("p (c r) -> p c r", c=4), mask4, ALU.mult).then_inc(masked, 1)

                def lo_part(dst, hi, hi_sem, tile, readers, signal):
                    after(dve, (hi_sem, tile, 1, 1), *readers)
                    dve.tensor_tensor(dst[:, :, :].rearrange("p k t -> p (k t)"), turn[:, :],
                                      hi[:, :, :].rearrange("p k t -> p (k t)").bitcast(F32), ALU.subtract).then_inc(signal, 1)

                def hidden_lo(tile, n, hi_sem, signal):
                    after(dve, (hi_sem, tile, n + 1, 4))
                    dve.tensor_tensor(HB[1][:, 2 * n:2 * n + 2, :].rearrange("p k t -> p (k t)"), HF[:, n % 2, :],
                                      HB[0][:, 2 * n:2 * n + 2, :].rearrange("p k t -> p (k t)").bitcast(F32),
                                      ALU.subtract).then_inc(signal, 1)

                def statistics(n, src, tile, source_sem, per):
                    after(dve, (source_sem, tile, per, per), own=True)
                    for g in range(TA):
                        ins = dve.bn_stats(bn[n][:, g, :], src[:, g, :])
                    ins.then_inc(bn_done[n], 1)
                    after(dve, (bn_done[n], tile, 1, 1), own=True)
                    for g in range(TA):
                        ins = dve.bn_aggr(mv[n][:, g, :], bn[n][:, g, :])
                    ins.then_inc(stats[n], 1)

                def normalise(dst, src, n, r, signal):
                    for g in range(TA):
                        ins = dve.tensor_scalar(dst[:, g, :], src[:, g, :], mv[n][:, g, 0:1], r[:, g:g + 1],
                                                ALU.subtract, ALU.mult)
                    ins.then_inc(signal, 1)

                def work(*steps):
                    for kind, n in steps:
                        if kind == "mask" and live(b):
                            masks(n)
                        elif kind == "hidden" and live(m):
                            hidden_lo(m, n, h_hi, h_lo)

                if live(m):
                    after(dve, (scale["x2"], m, 2, 2), (res_ready, m, 1, 1))
                    normalise(X2, X2, "x2", rs["x2"], z2_ready)
                work(("mask", 0), ("mask", 1))
                if live(m):
                    lo_part(Z2T[1], Z2T[0], z2h, m, [(fc_ready, m - 1, 4, 4)], z2l)
                if live(e):
                    after(dve, (w2_ready, e, 1, 1), (x3b_ready, e, 1, 1), (stored, e - 1, 32, 32))
                    dve.tensor_tensor(OUTB[:].rearrange("p a c -> p (a c)"), rows[:, :], X3B[:].rearrange("p a c -> p (a c)"),
                                      ALU.add).then_inc(out_ready, 1)
                work(("mask", 2), ("mask", 3), ("mask", 4))
                if live(q):
                    lo_part(ZT[1], ZT[0], zh, q, [(vqk_ready, q - 1, 3, 3)], zl)
                if live(f):
                    after(dve, (scale["x3"], f, 2, 2), (z3_turned, f - 1, 1, 1))
                    normalise(Z3, X3, "x3", rs["x3"], z3_ready)
                work(("mask", 5), ("hidden", 0), ("mask", 6), ("hidden", 1), ("mask", 7), ("hidden", 2), ("hidden", 3))
                if live(b):
                    statistics("xc", XC, b, xc_loaded, 32)
                if live(f):
                    lo_part(Z3T[1], Z3T[0], z3h, f, [(w1_ready, f - 1, 4, 4)], z3l)

                def elu(t):
                    after(dve, (qk_act, q, t + 1, 2))
                    dve.scalar_tensor_tensor(EXPRELU[:, t, :], EXPRELU[:, t, :], 1.0, EXPRELU[:, 2 + t, :],
                                             ALU.min, ALU.add).then_inc(qk_made, 1)

                if live(a):
                    statistics("x", X, a, x_loaded, 16)
                if peeled:
                    prepare(IN_MIDDLE.get(i, ()))
                def invert(g):
                    after(dve, (den_moved, b, 64, 64))
                    dve.reciprocal(DD[:, 2 * g:2 * g + 2, :, :].rearrange("p j m t -> p (j m t)"),
                                   DD[:, 2 * g:2 * g + 2, :, :].rearrange("p j m t -> p (j m t)")).then_inc(den_inverted, 1)

                if live(q):
                    elu(0)
                if live(b):
                    invert(0)
                if live(q):
                    elu(1)
                if live(b):
                    invert(1)
                    for g in range(TA):
                        after(dve, (num_moved, b, 64, 64), (den_inverted, b, g + 1, 2), (at_hi, b - 1, 1, 1), (at_lo, b - 1, 1, 1))
                        dve.tensor_tensor(AT[:, g, :, :].rearrange("p m (j t) -> p j m t", j=2), NN[:, 2 * g:2 * g + 2, :, :],
                                          DD[:, 2 * g:2 * g + 2, :, :], ALU.mult).then_inc(at_made, 1)
                if live(m):
                    after(dve, (proj_ready, m, 1, 1), (res_ready, m, 1, 1), (x3b_ready, m - 1, 1, 1), (z3_ready, m - 1, 1, 1))
                    dve.tensor_tensor(X3[:].rearrange("p a c -> p (a c)"), rows[:, :], RES[:].rearrange("p a c -> p (a c)"),
                                      ALU.add).then_inc(x3_ready, 1)
                if live(b):
                    after(dve, (scale["xc"], b, 2, 2), (x2_ready, b - 1, 1, 1))
                    normalise(Y, XC, "xc", rs["xc"], y_ready)
                    after(dve, (at_hi, b, 1, 1), (o_ready, b - 1, 1, 1))
                    dve.tensor_tensor(ATL[:].rearrange("p g m t -> p (g m t)"), AT[:].rearrange("p g m t -> p (g m t)"),
                                      ATH[:].rearrange("p g m t -> p (g m t)").bitcast(F32), ALU.subtract).then_inc(at_lo, 1)
                if live(q):
                    for t, moved in enumerate((q_moved, k_moved)):
                        after(dve, (qk_hi, q, t + 1, 2), (moved, q - 1, 96, 96))
                        dve.tensor_tensor(QKL[t][:, :, :].rearrange("p g n -> p (g n)"), EXPRELU[:, t, :],
                                          QKH[t][:, :, :].rearrange("p g n -> p (g n)").bitcast(F32),
                                          ALU.subtract).then_inc(qk_lo, 1)
                if live(f):
                    hidden_lo(f, 0, g_hi, g_lo)
                    hidden_lo(f, 1, g_hi, g_lo)
                if live(b):
                    after(dve, (o_ready, b, 1, 1), (yb_ready, b, 1, 1), (z2_turned, b - 1, 1, 1))
                    dve.tensor_tensor(X2[:].rearrange("p a c -> p (a c)"), rows[:, :], Y[:].rearrange("p a c -> p (a c)"),
                                      ALU.add).then_inc(x2_ready, 1)
                if live(b):
                    statistics("x2", X2, b, x2_ready, 1)
                if live(f):
                    hidden_lo(f, 2, g_hi, g_lo)
                    hidden_lo(f, 3, g_hi, g_lo)
                if live(m):
                    statistics("x3", X3, m, x3_ready, 1)
                if live(a):
                    after(dve, (scale["x"], a, 7, 7))
                    normalise(X, X, "x", rz, z_ready)

            run(dve, body)


def kernel(**inputs):
    import numpy as np
    import concourse.bacc as bacc
    from concourse.bass_utils import run_bass_kernel_spmd

    def channels(w, axis):
        w = np.moveaxis(np.asarray(w), axis, 0)
        w = w.reshape((H // 2, 2, D) + w.shape[1:])
        w = np.moveaxis(w, 0, 2).reshape((C,) + w.shape[3:])
        return np.ascontiguousarray(np.moveaxis(w, 0, axis))

    def columns(v):
        return np.ascontiguousarray(np.asarray(v).reshape(-1, P).T)

    g = lambda name: np.asarray(inputs["L0_" + name])
    qkv = ("q", "k", "v")
    r = np.arange(P)
    arrays = {
        "x": np.ascontiguousarray(g("attn_x").reshape(T, C)),
        "wqkv": np.ascontiguousarray(np.concatenate([channels(g(f"attn_{n}_w"), 0).T for n in qkv], axis=1)),
        "bqkv": np.ascontiguousarray(np.concatenate([columns(channels(g(f"attn_{n}_b"), 0)) for n in qkv], axis=1)),
        "ln1w": columns(g("attn_ln1_w")), "ln1b": columns(g("attn_ln1_b")),
        "wo": np.ascontiguousarray(channels(g("attn_o_w"), 1).T), "bo": g("attn_o_b"),
        "ln2w": columns(g("attn_ln2_w")), "ln2b": columns(g("attn_ln2_b")),
        "wfc": np.ascontiguousarray(g("attn_fc_w").T), "bfc": columns(g("attn_fc_b")),
        "wproj": np.ascontiguousarray(g("attn_proj_w").T), "bproj": g("attn_proj_b"),
        "w1": np.ascontiguousarray(g("ffn_W1")), "b1": columns(g("ffn_b1")),
        "w2": np.ascontiguousarray(g("ffn_W2")), "b2": g("ffn_b2"),
        "ident": np.eye(P, dtype=np.float32),
        "mask": (r[:, None] % CH == r[None, :] % CH).astype(np.float32),
    }
    nc = bacc.Bacc("TRN2", target_bir_lowering=False, num_devices=1)
    args = [nc.dram_tensor(f"in_{name}", a.shape, mybir.dt.from_np(a.dtype), kind="ExternalInput").ap() for name, a in arrays.items()]
    result = nc.dram_tensor("result", (T, C), F32, kind="ExternalOutput").ap()
    build(nc, *args, result)
    got = run_bass_kernel_spmd(nc, [{f"in_{n}": a for n, a in arrays.items()}], core_ids=[0])
    return got.results[0]["result"].reshape(8, T // 8, C)
```

```python
from contextlib import ExitStack

import concourse.bass as bass
from concourse import mybir

F32 = mybir.dt.float32
F32R = mybir.dt.float32r
ALU = mybir.AluOpType
ACT = mybir.ActivationFunctionType

P = 128
T = 8192
C = 256
KC = C // P
F = 1024
FB = F // P
H, D = 16, 16
TT = 256
TA = TT // P
NT = T // TT
CH = P // H
NCH = P // CH
EPS = 1e-5
DEPTH = 5


def after(eng, *needs, own=False):
    values = []
    for sem, tile, k, per in needs:
        if isinstance(tile, int):
            if tile >= 0:
                values.append((sem, min(tile, NT - 1) * per + (k if tile < NT else per)))
        else:
            values.append((sem, eng.snap(tile * per + k)))
    for sem, value in values:
        eng.wait_ge(sem, value)
        if own and not isinstance(value, int):
            eng.nop(nofuse=True)


def live(tile):
    return not isinstance(tile, int) or 0 <= tile < NT


def run(eng, body):
    for i in range(DEPTH + 1):
        body(i, True)
    with eng.Fori(DEPTH + 1, NT) as i:
        body(i, False)
    for i in range(NT, NT + DEPTH):
        body(i, True)


def build(nc, x, wqkv, bqkv, ln1w, ln1b, wo, bo, ln2w, ln2b, wfc, bfc, wproj, bproj, w1, b1, w2, b2, ident_in, mask_in, out):
    with ExitStack() as ctx:
        def sb(name, shape, dt=F32):
            return ctx.enter_context(nc.sbuf_tensor(name, shape, dt))

        def sem(name):
            return ctx.enter_context(nc.semaphore(name))

        WQKV = [sb(f"wqkv_{p}", [P, KC, 3 * C], F32R) for p in "hl"]
        WO = [sb(f"wo_{p}", [P, KC, C], F32R) for p in "hl"]
        WFC = [sb(f"wfc_{p}", [P, KC, F], F32R) for p in "hl"]
        WPROJ = [sb(f"wproj_{p}", [P, FB, C], F32R) for p in "hl"]
        W1 = [sb(f"w1_{p}", [P, KC, F], F32R) for p in "hl"]
        W2 = [sb(f"w2_{p}", [P, FB, C], F32R) for p in "hl"]
        ident = sb("ident", [P, P])
        mask = sb("mask", [P, P])
        bqkv_raw = sb("bqkv_raw", [P, 6])
        bfc_raw = sb("bfc_raw", [P, FB])
        qkv_bias = sb("qkv_bias", [P, 6])
        fc_bias = sb("fc_bias", [P, FB])
        b1_sb = sb("b1_sb", [P, FB])
        ln1 = sb("ln1", [P, 2, KC])
        ln2 = sb("ln2", [P, 2, KC])
        bo_rows = sb("bo_rows", [P, C])
        bproj_rows = sb("bproj_rows", [P, C])
        b2_rows = sb("b2_rows", [P, C])
        minus_half = sb("minus_half", [P, TA])
        X = sb("X", [P, TA, C])
        XC = sb("XC", [P, TA, C])
        early = sb("early_rows", [P, 4, TA * C])
        late = sb("late_rows", [P, 4, TA * C])
        Y, X2, RES = (early[:, n, :].rearrange("p (a c) -> p a c", a=TA) for n in range(3))
        X3, Z3, X3B, OUTB = (late[:, n, :].rearrange("p (a c) -> p a c", a=TA) for n in range(4))
        ZT = [sb(f"zt_{p}", [P, KC, TT], F32R) for p in "hl"]
        Z2T = [sb(f"z2t_{p}", [P, KC, TT], F32R) for p in "hl"]
        Z3T = [sb(f"z3t_{p}", [P, KC, TT], F32R) for p in "hl"]
        HB = [sb(f"hidden_{p}", [P, FB, TT], F32R) for p in "hl"]
        HF = sb("hidden_f32", [P, 2, 2 * TT])
        EXPRELU = sb("exp_relu", [P, 4, TA * KC * P])
        QKH = [sb(f"{n}_hi", [P, TA, KC * P], F32R) for n in "qk"]
        QKL = [sb(f"{n}_lo", [P, TA, KC * P], F32R) for n in "qk"]
        VN = sb("VN", [P, TA, KC * P])
        QD = sb("QD", [P, H * P], F32R)
        KD = sb("KD", [P, H * P], F32R)
        VD = sb("VD", [P, H * P])
        VC = sb("VC", [P, TA * NCH, 2 * D])
        A = sb("A", [P, 4, 4 * P])
        ND = sb("ND", [P, H, 8, 8])
        NN = sb("NN", [P, 4, 2, 64])
        DD = sb("DD", [P, 4, 2, 64])
        AT = early[:, 3, :].rearrange("p (g m t) -> p g m t", g=TA, m=KC)
        ATH = sb("AT_hi", [P, TA, KC, P], F32R)
        ATL = sb("AT_lo", [P, TA, KC, P], F32R)
        bn = {n: sb(f"bn_{n}", [P, TA, 6]) for n in ("x", "xc", "x2", "x3")}
        mv = {n: sb(f"mv_{n}", [P, TA, 2]) for n in ("x", "xc", "x2", "x3")}
        ve = {n: sb(f"ve_{n}", [P, TA]) for n in ("x", "xc", "x2", "x3")}
        rs = {n: sb(f"rs_{n}", [P, TA]) for n in ("x", "xc", "x2", "x3")}
        sq = sb("sq", [P, TA])
        sv = sb("sv", [P, TA])
        se = sb("se", [P, TA])
        rz1 = sb("rz1", [P, TA])
        rz = sb("rz", [P, TA])

        def bank(name):
            return ctx.enter_context(nc.psum_tensor(name, [P, 512], F32))
        turn = bank("turn")
        wide = [bank("wide_a"), bank("wide_b")]
        rows = bank("rows")
        score = [bank("score_0"), bank("score_1")]
        summed = [bank("summed_0"), bank("summed_1")]

        first_loaded, others_loaded = sem("first_loaded"), sem("others_loaded")
        w_loaded = [sem(f"w_loaded_{n}") for n in range(7)]
        w_scaled, w_hi, w_lo, w_bias_sum, w_bias = (sem(n) for n in ("w_scaled", "w_hi", "w_lo", "w_bias_sum", "w_bias"))
        ones_set = sem("ones_set")
        x_loaded = sem("x_loaded")
        xc_loaded = sem("xc_loaded")
        bn_done = {n: sem(f"bn_done_{n}") for n in bn}
        stats = {n: sem(f"stats_{n}") for n in bn}
        scale = {n: sem(f"scale_{n}") for n in bn}
        z_ready, z2_ready, z3_ready = sem("z_ready"), sem("z2_ready"), sem("z3_ready")
        z_turned, z2_turned, z3_turned = sem("z_turned"), sem("z2_turned"), sem("z3_turned")
        zh, z2h, z3h = sem("zh"), sem("z2h"), sem("z3h")
        zl, z2l, z3l = sem("zl"), sem("z2l"), sem("z3l")
        vqk_ready = sem("vqk_ready")
        qk_act = sem("qk_act")
        v_act = sem("v_act")
        qk_made = sem("qk_made")
        qk_hi = sem("qk_hi")
        qk_lo = sem("qk_lo")
        q_moved, k_moved = sem("q_moved"), sem("k_moved")
        v_moved = sem("v_moved")
        v_turned = sem("v_turned")
        vc_ready = sem("vc_ready")
        scored = [sem("scored_0"), sem("scored_1")]
        masked = sem("masked")
        a_used = [sem("a_used_0"), sem("a_used_1")]
        nd_ready = sem("nd_ready")
        num_moved, den_moved = sem("num_moved"), sem("den_moved")
        den_inverted = sem("den_inverted")
        at_made = sem("at_made")
        at_hi, at_lo = sem("at_hi"), sem("at_lo")
        y_ready, yb_ready = sem("y_ready"), sem("yb_ready")
        xc_biased = sem("xc_biased")
        o_ready, x2_ready, res_ready = sem("o_ready"), sem("x2_ready"), sem("res_ready")
        fc_ready, gelu_made, h_hi, h_lo = sem("fc_ready"), sem("gelu_made"), sem("h_hi"), sem("h_lo")
        proj_ready, x3_ready, x3b_ready = sem("proj_ready"), sem("x3_ready"), sem("x3b_ready")
        w1_ready, relu_made, g_hi, g_lo = sem("w1_ready"), sem("relu_made"), sem("g_hi"), sem("g_lo")
        w2_ready, out_ready = sem("w2_ready"), sem("out_ready")
        stored = sem("stored")

        x_rows = x.rearrange("(n p a) c -> n p (a c)", p=P, a=TA)
        x_rows_c = x.rearrange("(n s jj i a) c -> n jj s i (a c)", s=8, jj=2, i=8, a=TA)
        out_rows_c = out.rearrange("(n s jj i a) c -> n jj s i (a c)", s=8, jj=2, i=8, a=TA)

        def flat(tile):
            return tile[:].rearrange({3: "p a b -> p (a b)", 4: "p a b c -> p (a b c)"}[len(tile.shape)])

        half = [FB // 2 * m for m in range(3)]
        rows_of = lambda w, a, b: w[P * a:P * b, :].rearrange("(k p) n -> p k n", p=P)
        FOLD_1 = (0, ln1, flat(EXPRELU), summed[0], bqkv_raw, qkv_bias, 6)
        FOLD_2 = (1, ln2, flat(A), rows, bfc_raw, fc_bias, FB)
        WEIGHTS = [
            (rows_of(wqkv, 0, KC), [w[:] for w in WQKV], VD[:, :], FOLD_1),
            (rows_of(wproj, 0, FB), [w[:] for w in WPROJ], flat(late), None),
            (rows_of(w1, 0, KC), [w[:] for w in W1], flat(early), None),
            (rows_of(wo, 0, KC), [w[:] for w in WO], flat(NN), None),
            (rows_of(w2, half[0], half[1]), [w[:, half[0]:half[1], :] for w in W2], flat(HF), None),
            (rows_of(w2, half[1], half[2]), [w[:, half[1]:half[2], :] for w in W2], flat(ND), None),
            (rows_of(wfc, 0, KC), [w[:] for w in WFC], flat(A), FOLD_2),
        ]
        WQKV_SPLIT, WPROJ_SPLIT, W1_SPLIT, WO_SPLIT, W2_SPLIT, WFC_SPLIT = 1, 2, 3, 4, 6, 7

        def shaped(n, buffer):
            _, blocks, width = WEIGHTS[n][0].shape
            return buffer[:, 0:blocks * width].rearrange("p (k n) -> p k n", k=blocks)

        def staged(n):
            return shaped(n, WEIGHTS[n][2])

        def scaled(n):
            fold = WEIGHTS[n][3]
            return shaped(n, fold[2]) if fold else staged(n)

        IN_FRONT = {1: (0,), 2: (3, 4, 5, 6)}
        IN_MIDDLE = {1: (1, 2)}

        block = ctx.enter_context(nc.Block())

        @block.sync
        def _(sp):
            first = [(ident[:], ident_in), (ln1[:, 0, :], ln1w), (ln1[:, 1, :], ln1b), (bqkv_raw[:], bqkv)]
            others = [(mask[:], mask_in), (ln2[:, 0, :], ln2w), (ln2[:, 1, :], ln2b), (bfc_raw[:], bfc), (b1_sb[:], b1),
                      (bo_rows[:], bo.partition_broadcast(P)), (bproj_rows[:], bproj.partition_broadcast(P)),
                      (b2_rows[:], b2.partition_broadcast(P))]

            def load_weight(n):
                sp.dma_start(staged(n), WEIGHTS[n][0]).then_inc(w_loaded[n], 16)

            sp.dma_start(X[:, :, :].rearrange("p a c -> p (a c)"), x_rows[0]).then_inc(x_loaded, 16)
            load_weight(0)
            for dst, src in first:
                sp.dma_start(dst, src).then_inc(first_loaded, 16)
            load_weight(1)
            for dst, src in others:
                sp.dma_start(dst, src).then_inc(others_loaded, 16)
            for n in range(2, len(WEIGHTS)):
                load_weight(n)

            def body(i, peeled):
                a, q, c, e = i, i - 1, i - 2, i - 5
                if live(c):
                    after(sp, (res_ready, c - 1, 1, 1), own=True)
                    for jj in range(2):
                        sp.dma_start(XC[64 * jj:64 * jj + 64, :, :].rearrange("p a c -> p (a c)"),
                                     x_rows_c[c, jj]).then_inc(xc_loaded, 16)
                if live(a) and not (peeled and i == 0):
                    after(sp, (z_turned, a - 1, 1, 1), own=True)
                    sp.dma_start(X[:, :, :].rearrange("p a c -> p (a c)"), x_rows[a]).then_inc(x_loaded, 16)
                if live(e):
                    after(sp, (out_ready, e, 1, 1), own=True)
                    for jj in range(2):
                        sp.dma_start(out_rows_c[e, jj],
                                     OUTB[64 * jj:64 * jj + 64, :, :].rearrange("p a c -> p (a c)")).then_inc(stored, 16)
                if live(c):
                    after(sp, (nd_ready, c, 2, 2), (at_made, c - 1, 2, 2), own=True)
                    for dst, part, moved in ((DD, D, den_moved), (NN, 0, num_moved)):
                        for j in range(4):
                            sp.dma_start(dst[:, j, :, :].rearrange("p m t -> p (m t)"),
                                         ND[32 * j + part:32 * j + part + D, :, :, :].rearrange("p h s i -> p (h s i)"))\
                              .then_inc(moved, 16)
                if live(q):
                    after(sp, (v_act, q, 1, 1), (v_turned, q - 1, 1, 1), own=True)
                    for g in range(TA):
                        sp.dma_start(VD[D * g:D * g + D, :], VN[:, g, :]).then_inc(v_moved, 16)
                    after(sp, (scored[0], q - 1, 4, 4), (scored[1], q - 1, 4, 4), own=True)
                    for t, (dst, his, moved) in enumerate(((QD, (0, 2), q_moved), (KD, (0, 1), k_moved))):
                        after(sp, (qk_hi, q, t + 1, 2), own=True)
                        for g in range(TA):
                            for h in his:
                                sp.dma_start(dst[64 * g + D * h:64 * g + D * h + D, :].bitcast(F32),
                                             QKH[t][:, g, :].bitcast(F32)).then_inc(moved, 16)
                    for t, (dst, lo, moved) in enumerate(((QD, 1, q_moved), (KD, 2, k_moved))):
                        after(sp, (qk_lo, q, t + 1, 2), own=True)
                        for g in range(TA):
                            sp.dma_start(dst[64 * g + D * lo:64 * g + D * lo + D, :].bitcast(F32),
                                         QKL[t][:, g, :].bitcast(F32)).then_inc(moved, 16)

            run(sp, body)
            sp.wait_ge(stored, 32 * NT)

        @block.tensor
        def _(pe):
            pe.wait_ge(first_loaded, 16 * 4)

            def shift_sums(n):
                _, ln, _, bank, _, _, blocks = WEIGHTS[n][3]
                pe.wait_ge(w_loaded[n], 16)
                for m in range(blocks):
                    for k in range(KC):
                        mm = pe.matmul(bank[:, m:m + 1], staged(n)[:, k, P * m:P * m + P], ln[:, 1, k:k + 1],
                                       start=(k == 0), stop=(k == KC - 1))
                mm.then_inc(w_bias_sum, 1)

            def product(dst, hi_lo_w, hi_lo_x, parts):
                passes = [(0, 0), (1, 0), (0, 1)]
                n = len(parts)
                for k, (w, xx) in enumerate(parts):
                    for m, (pw, px) in enumerate(passes):
                        mm = pe.matmul(dst, w(hi_lo_w[pw]), xx(hi_lo_x[px]), start=(k == 0 and m == 0),
                                       stop=(k == n - 1 and m == 2))
                return mm

            def turn_rows(z):
                for g in range(TA):
                    for k in range(KC):
                        mm = pe.transpose(turn[:, TT * k + P * g:TT * k + P * g + P], z[:, g, P * k:P * k + P], ident[:])
                return mm

            def blocks_of(w, zt, first, dst):
                for b in range(2):
                    lo = P * (first + b)
                    mm = product(dst[:, TT * b:TT * b + TT], w, zt,
                                 [(lambda v, k=k: v[:, k, lo:lo + P], lambda v, k=k: v[:, k, :]) for k in range(KC)])
                return mm

            def token_rows(act, w, count, in_front=None, groups=range(TA)):
                for g in groups:
                    dst = rows[:, C * g:C * g + C]
                    for k in range(count):
                        if in_front:
                            in_front(g, k)
                        for m, (pa, pw) in enumerate([(0, 0), (1, 0), (0, 1)]):
                            mm = pe.matmul(dst, act(pa, k, g), w[pw][:, k, :], start=(k == 0 and m == 0),
                                           stop=(k == count - 1 and m == 2))
                return mm

            def chunks(p):
                for c, i in enumerate((2 * p, 2 * p + 1, 8 + 2 * p, 8 + 2 * p + 1)):
                    for a in range(TA):
                        yield a, c, i, 2 * a + i // 8, i % 4

            def body(i, peeled):
                q, b, m, f, e = i - 1, i - 2, i - 3, i - 4, i - 5

                def scores(p):
                    if p == 0:
                        after(pe, (q_moved, b, 96, 96), (k_moved, b, 96, 96), (masked, b - 1, 8, 8))
                    else:
                        after(pe, (masked, b, 2 * p, 8))
                    for g, c, ch, _, _ in chunks(p):
                        mm = pe.matmul(score[g][:, P * c:P * c + P], KD[64 * g:64 * g + 3 * D, ch:H * P:NCH],
                                       QD[64 * g:64 * g + 3 * D, ch:H * P:NCH], start=True, stop=True)
                        if c == 3:
                            mm.then_inc(scored[g], 1)

                def weighted(p):
                    if p == 0:
                        after(pe, (vc_ready, b, 1, 1), (masked, b, 2, 8), (nd_ready, b - 1, 1, 2))
                    elif p == 2:
                        after(pe, (masked, b, 6, 8), (nd_ready, b - 1, 2, 2))
                    else:
                        after(pe, (masked, b, 2 * p + 2, 8))
                    for g, c, ch, j, place in chunks(p):
                        mm = pe.matmul(summed[p // 2][32 * j:32 * j + 32, P * place:P * place + P], VC[:, NCH * g + ch, :],
                                       A[:, 2 * (p % 2) + g, P * c:P * c + P], start=True, stop=True)
                        if c == 3:
                            mm.then_inc(a_used[g], 1)

                def turn_z2():
                    extra = [(z3l, f - 1, 1, 1)] if peeled else []
                    after(pe, (z2_ready, m, 1, 1), (vc_ready, b, 1, 1), *extra)
                    turn_rows(X2).then_inc(z2_turned, 1)

                def attend(p):
                    if live(b):
                        weighted(p)
                        if p < 3:
                            scores(p + 1)

                for g in range(TA):
                    if live(e):
                        if g == 0:
                            extra = [(x3_ready, m - 1, 1, 1), (out_ready, e - 1, 1, 1)] if peeled else []
                            after(pe, (x2_ready, b - 1, 1, 1), *extra)
                        if peeled:
                            pe.wait_ge(w_lo, W2_SPLIT)

                        def in_front(g, k):
                            if g == 0 and k % 2 == 0:
                                after(pe, (g_lo, e, k // 2 + 1, 4))
                            elif g == 1 and k == FB // 2 and live(m):
                                turn_z2()
                        mm = token_rows(lambda part, k, g: HB[part][:, k, P * g:P * g + P], W2, FB, in_front, [g])
                        if g == TA - 1:
                            mm.then_inc(w2_ready, 1)
                    if g == 0 and live(b):
                        scores(0)
                if live(m) and not live(e):
                    turn_z2()
                attend(0)
                if live(q):
                    extra = [(vc_ready, q - 1, 1, 1)] if peeled else []
                    after(pe, (z_ready, q, 1, 1), (z2l, m, 1, 1), *extra)
                    turn_rows(X).then_inc(z_turned, 1)
                if peeled and i == 1:
                    shift_sums(0)
                for n, pair in enumerate((1, None, 2, 3)):
                    if live(m):
                        if n == 0:
                            extra = [(qk_act, q - 1, 2, 2), (gelu_made, m - 1, 4, 4)] if peeled else []
                            after(pe, (z2l, m, 1, 1), (relu_made, f - 1, 4, 4), *extra)
                        elif n >= 2:
                            after(pe, (gelu_made, m, n - 1, 4))
                        if peeled:
                            pe.wait_ge(w_lo, WFC_SPLIT)
                        blocks_of(WFC, Z2T, 2 * n, wide[n % 2]).then_inc(fc_ready, 1)
                    if pair:
                        attend(pair)
                if live(f):
                    extra = [(z2l, m, 1, 1), (z3l, f - 1, 1, 1)] if peeled else []
                    after(pe, (z3_ready, f, 1, 1), (zl, q, 1, 1), *extra)
                    turn_rows(Z3).then_inc(z3_turned, 1)
                if live(q):
                    for n, t in enumerate((2, 0, 1)):
                        if n == 0:
                            extra = [(qk_act, q - 1, 2, 2)] if peeled else []
                            after(pe, (zl, q, 1, 1), (gelu_made, m, 3, 4), *extra)
                        elif n == 1:
                            after(pe, (gelu_made, m, 4, 4))
                        else:
                            after(pe, (v_act, q, 1, 1))
                        if peeled:
                            pe.wait_ge(w_lo, WQKV_SPLIT)
                        blocks_of(WQKV, ZT, 2 * t, wide[n % 2]).then_inc(vqk_ready, 1)
                if live(m):
                    extra = [(x2_ready, b - 1, 1, 1)] if peeled else []
                    after(pe, (out_ready, e, 1, 1), *extra)

                    def h_block(g, k):
                        if g == 0 and k % 2 == 0:
                            after(pe, (h_lo, m, k // 2 + 1, 4))
                    if peeled:
                        pe.wait_ge(w_lo, WPROJ_SPLIT)
                    token_rows(lambda part, k, g: HB[part][:, k, P * g:P * g + P], WPROJ, FB, h_block).then_inc(proj_ready, 1)

                def output_projection():
                    if not live(b):
                        return
                    after(pe, (at_hi, b, 1, 1), (at_lo, b, 1, 1), (x3_ready, m, 1, 1))
                    if peeled:
                        pe.wait_ge(w_lo, WO_SPLIT)
                    token_rows(lambda part, k, g: (ATH, ATL)[part][:, g, k, :], WO, KC).then_inc(o_ready, 1)
                if live(f):
                    for n in range(4):
                        if n == 3:
                            output_projection()
                        if n == 0:
                            extra = [(gelu_made, m, 4, 4), (relu_made, f - 1, 4, 4)] if peeled else []
                            after(pe, (z3l, f, 1, 1), (qk_act, q, 1, 2), *extra)
                        elif n == 1:
                            after(pe, (qk_act, q, 2, 2))
                        else:
                            after(pe, (relu_made, f, n - 1, 4))
                        if peeled:
                            pe.wait_ge(w_lo, W1_SPLIT)
                        blocks_of(W1, Z3T, 2 * n, wide[(n + 1) % 2]).then_inc(w1_ready, 1)
                if not live(f):
                    output_projection()
                if live(q):
                    extra = [(zl, q, 1, 1)] if peeled else []
                    after(pe, (v_moved, q, 32, 32), (z3l, f, 1, 1), *extra, own=True)
                    for ch in range(NCH):
                        mm = pe.transpose(turn[:, TA * D * ch:TA * D * ch + TA * D], VD[0:TA * D, ch:H * P:NCH],
                                          ident[0:TA * D, 0:TA * D])
                    mm.then_inc(v_turned, 1)
                if peeled and i == 1:
                    pe.wait_ge(others_loaded, 16 * 8)
                    shift_sums(6)

            run(pe, body)

        @block.scalar
        def _(act):
            def prepare(weights):
                for n in weights:
                    _, w, _, fold = WEIGHTS[n]
                    act.wait_ge(w_loaded[n], 16)
                    if fold:
                        act.wait_ge(w_scaled, fold[0] + 1)
                    act.activation(w[0], scaled(n), ACT.Copy).then_inc(w_hi, 1)

            def body(i, peeled):
                q, b, m, f = i - 1, i - 2, i - 3, i - 4
                if peeled:
                    prepare(IN_FRONT.get(i, ()))

                def sums(u):
                    moved = [(num_moved, b - 1, 64, 64), (den_moved, b - 1, 64, 64)] if u == 0 else []
                    after(act, (a_used[0], b, 2 * u + 2, 4), (a_used[1], b, 2 * u + 2, 4), *moved)
                    act.activation(ND[:, :, :, 4 * u:4 * u + 4].rearrange("p h s i -> p i h s"),
                                   summed[u][:, :].rearrange("p (i h s) -> p i h s", i=4, h=H), ACT.Copy).then_inc(nd_ready, 1)

                def hi_part(dst, turned, tile, readers, signal):
                    after(act, (turned, tile, 1, 1), *readers)
                    act.activation(dst[:, :, :].rearrange("p k t -> p (k t)"), turn[:, :], ACT.Copy).then_inc(signal, 1)

                def hidden_hi(tile, n, made, readers, signal):
                    after(act, (made, tile, n + 1, 4), *(readers if n == 0 else []))
                    act.activation(HB[0][:, 2 * n:2 * n + 2, :].rearrange("p k t -> p (k t)"), HF[:, n % 2, :],
                                   ACT.Copy).then_inc(signal, 1)

                if live(m):
                    hi_part(Z2T[0], z2_turned, m, [(fc_ready, m - 1, 4, 4)], z2h)
                if live(q):
                    hi_part(ZT[0], z_turned, q, [(vqk_ready, q - 1, 3, 3)], zh)
                if peeled:
                    prepare(IN_MIDDLE.get(i, ()))
                if peeled and i == 3:
                    act.wait_ge(w_bias, 2)
                    act.wait_ge(others_loaded, 16 * 8)
                for n in range(4):
                    if live(m):
                        extra = [(h_lo, m - 1, 4, 4)] if peeled and n < 2 else []
                        free = (g_lo, f - 1, 4, 4) if n < 2 else (h_lo, m, n - 1, 4)
                        after(act, (fc_ready, m, n + 1, 4), free, *extra)
                        for k in range(2):
                            ins = act.activation(HF[:, n % 2, TT * k:TT * k + TT], wide[n % 2][:, TT * k:TT * k + TT], ACT.Gelu,
                                                 bias=fc_bias[:, 2 * n + k:2 * n + k + 1])
                        ins.then_inc(gelu_made, 1)
                        extra = [(proj_ready, m - 1, 1, 1)] if peeled else []
                        hidden_hi(m, n, gelu_made, [(w2_ready, f - 1, 1, 1), *extra], h_hi)
                    if live(b) and n in (2, 3):
                        sums(n - 2)
                if peeled and i == 1:
                    act.wait_ge(w_bias, 1)
                if live(q):
                    after(act, (vqk_ready, q, 1, 3), (v_moved, q - 1, 32, 32))
                    for k in range(KC):
                        ins = act.activation(VN[:, :, :].rearrange("p g (m t) -> p g m t", m=KC)[:, :, k, :],
                                             wide[0][:, TT * k:TT * k + TT].rearrange("p (g t) -> p g t", g=TA), ACT.Identity,
                                             bias=qkv_bias[:, 4 + k:5 + k])
                    ins.then_inc(v_act, 1)
                if live(f):
                    hi_part(Z3T[0], z3_turned, f, [(w1_ready, f - 1, 4, 4)], z3h)
                if live(q):
                    for t in range(2):
                        after(act, (vqk_ready, q, t + 2, 3), (qk_lo, q - 1, t + 1, 2))
                        for s, fn in ((0, ACT.Exp), (2, ACT.Relu)):
                            for k in range(KC):
                                ins = act.activation(
                                    EXPRELU[:, t + s, :].rearrange("p (g m t) -> p g m t", g=TA, m=KC)[:, :, k, :],
                                    wide[(t + 1) % 2][:, TT * k:TT * k + TT].rearrange("p (g t) -> p g t", g=TA), fn,
                                    bias=qkv_bias[:, 2 * t + k:2 * t + k + 1])
                        ins.then_inc(qk_act, 1)
                    for t, moved in enumerate((q_moved, k_moved)):
                        after(act, (qk_made, q, t + 1, 2), (moved, q - 1, 96, 96))
                        act.activation(QKH[t][:, :, :].rearrange("p g n -> p (g n)"), EXPRELU[:, t, :],
                                       ACT.Copy).then_inc(qk_hi, 1)
                for n in range(4):
                    if live(f):
                        extra = [(g_lo, f - 1, 4, 4)] if peeled and n < 2 else []
                        free = (h_lo, m, n + 3, 4) if n < 2 else (g_lo, f, n - 1, 4)
                        after(act, (w1_ready, f, n + 1, 4), free, *extra)
                        for k in range(2):
                            ins = act.activation(HF[:, n % 2, TT * k:TT * k + TT],
                                                 wide[(n + 1) % 2][:, TT * k:TT * k + TT], ACT.Relu,
                                                 bias=b1_sb[:, 2 * n + k:2 * n + k + 1])
                        ins.then_inc(relu_made, 1)
                    if live(b) and n == 0:
                        after(act, (at_made, b, 2, 2), (o_ready, b - 1, 1, 1))
                        act.activation(ATH[:, :, :, :].rearrange("p g m t -> p (g m t)"),
                                       AT[:, :, :, :].rearrange("p g m t -> p (g m t)"), ACT.Copy).then_inc(at_hi, 1)
                    if live(f):
                        extra = [(w2_ready, f - 1, 1, 1)] if peeled else []
                        hidden_hi(f, n, relu_made, [(proj_ready, m, 1, 1), *extra], g_hi)
                if live(q):
                    after(act, (v_turned, q, 1, 1), (a_used[0], q - 1, 4, 4), (a_used[1], q - 1, 4, 4))
                    act.activation(VC[:, :, 0:D].rearrange("p (g c) e -> p c g e", g=TA),
                                   turn[:, :].rearrange("p (c g e) -> p c g e", g=TA, e=D), ACT.Copy).then_inc(vc_ready, 1)

            run(act, body)

        @block.gpsimd
        def _(pool):
            pool.memset(minus_half[:], -0.5).then_inc(ones_set, 1)
            pool.memset(VC[:, :, D:2 * D], 1.0).then_inc(ones_set, 1)
            pool.wait_ge(ones_set, 2)

            def body(i, peeled):
                a, b, m, f = i, i - 2, i - 3, i - 4
                if peeled and i == 2:
                    pool.wait_ge(others_loaded, 16 * 8)

                def inverse_root(n, tile, per):
                    after(pool, (stats[n], tile, 1, 1), own=True)
                    pool.tensor_scalar(ve[n][:], mv[n][:, :, 1], EPS, None, ALU.add).then_inc(scale[n], 1)
                    after(pool, (scale[n], tile, 1, per), own=True)
                    pool.tensor_tensor(rs[n][:], ve[n][:], minus_half[:], ALU.pow).then_inc(scale[n], 1)

                if live(b):
                    inverse_root("xc", b, 2)
                if live(a):
                    inverse_root("x", a, 7)
                    after(pool, (scale["x"], a, 2, 7), own=True)
                    pool.tensor_tensor(sq[:], rs["x"][:], rs["x"][:], ALU.mult).then_inc(scale["x"], 1)
                    after(pool, (scale["x"], a, 3, 7), own=True)
                    pool.tensor_tensor(sv[:], sq[:], mv["x"][:, :, 1], ALU.mult).then_inc(scale["x"], 1)
                    after(pool, (scale["x"], a, 4, 7), own=True)
                    pool.tensor_scalar(se[:], sv[:], EPS, None, ALU.add).then_inc(scale["x"], 1)
                    after(pool, (scale["x"], a, 5, 7), own=True)
                    pool.tensor_tensor(rz1[:], se[:], minus_half[:], ALU.pow).then_inc(scale["x"], 1)
                    after(pool, (scale["x"], a, 6, 7), own=True)
                    pool.tensor_tensor(rz[:], rz1[:], rs["x"][:], ALU.mult).then_inc(scale["x"], 1)
                if live(b):
                    after(pool, (y_ready, b, 1, 1), own=True)
                    for g in range(TA):
                        ins = pool.tensor_tensor(Y[:, g, :], Y[:, g, :], bo_rows[:], ALU.add)
                    ins.then_inc(yb_ready, 1)
                    for g in range(TA):
                        ins = pool.tensor_tensor(XC[:, g, :], XC[:, g, :], bproj_rows[:], ALU.add)
                    ins.then_inc(xc_biased, 1)
                    inverse_root("x2", b, 2)
                    after(pool, (x2_ready, b, 1, 1), (xc_biased, b, 1, 1), (x3_ready, m, 1, 1), own=True)
                    pool.tensor_tensor(RES[:].rearrange("p a c -> p (a c)"), X2[:].rearrange("p a c -> p (a c)"),
                                       XC[:].rearrange("p a c -> p (a c)"), ALU.add).then_inc(res_ready, 1)
                if live(m):
                    inverse_root("x3", m, 2)
                    after(pool, (x3_ready, m, 1, 1), (out_ready, f, 1, 1), own=True)
                    for g in range(TA):
                        ins = pool.tensor_tensor(X3B[:, g, :], X3[:, g, :], b2_rows[:], ALU.add)
                    ins.then_inc(x3b_ready, 1)

            run(pool, body)

        @block.vector
        def _(dve):
            def prepare(weights):
                for n in weights:
                    _, w, _, fold = WEIGHTS[n]
                    dve.wait_ge(w_loaded[n], 16)
                    if fold:
                        u, ln = fold[:2]
                        dve.wait_ge(first_loaded, 16 * 4)
                        if u > 0:
                            dve.wait_ge(others_loaded, 16 * 8)
                            bias(n)
                        for k in range(KC):
                            ins = dve.tensor_scalar(scaled(n)[:, k, :], staged(n)[:, k, :], ln[:, 0, k:k + 1], None, ALU.mult)
                        ins.then_inc(w_scaled, 1)
                        dve.wait_ge(w_scaled, u + 1)
                    dve.wait_ge(w_hi, n + 1)
                    dve.tensor_tensor(w[1], scaled(n), w[0].bitcast(F32), ALU.subtract).then_inc(w_lo, 1)
                    dve.wait_ge(w_lo, n + 1)

            def bias(n):
                u, _, _, bank, raw, dst, blocks = WEIGHTS[n][3]
                dve.wait_ge(w_bias_sum, u + 1)
                dve.tensor_tensor(dst[:], bank[:, 0:blocks], raw[:], ALU.add).then_inc(w_bias, 1)

            mask4 = bass.AP(mask[:].tensor, 0, [[P, P], [0, 4], [1, P]])

            def body(i, peeled):
                a, q, b, m, f, e = i, i - 1, i - 2, i - 3, i - 4, i - 5
                if peeled:
                    prepare(IN_FRONT.get(i, ()))

                def masks(n):
                    g, p = n % 2, n // 2
                    used = (a_used[g], b, p - 1, 4) if p >= 2 else (a_used[g], b - 1, p + 3, 4)
                    after(dve, (scored[g], b, p + 1, 4), used)
                    dve.tensor_tensor(A[:, n % 4, :].rearrange("p (c r) -> p c r", c=4),
                                      score[n % 2][:, :].rearrange("p (c r) -> p c r", c=4), mask4, ALU.mult).then_inc(masked, 1)

                def lo_part(dst, hi, hi_sem, tile, readers, signal):
                    after(dve, (hi_sem, tile, 1, 1), *readers)
                    dve.tensor_tensor(dst[:, :, :].rearrange("p k t -> p (k t)"), turn[:, :],
                                      hi[:, :, :].rearrange("p k t -> p (k t)").bitcast(F32), ALU.subtract).then_inc(signal, 1)

                def hidden_lo(tile, n, hi_sem, signal):
                    after(dve, (hi_sem, tile, n + 1, 4))
                    dve.tensor_tensor(HB[1][:, 2 * n:2 * n + 2, :].rearrange("p k t -> p (k t)"), HF[:, n % 2, :],
                                      HB[0][:, 2 * n:2 * n + 2, :].rearrange("p k t -> p (k t)").bitcast(F32),
                                      ALU.subtract).then_inc(signal, 1)

                def statistics(n, src, tile, source_sem, per):
                    after(dve, (source_sem, tile, per, per), own=True)
                    for g in range(TA):
                        ins = dve.bn_stats(bn[n][:, g, :], src[:, g, :])
                    ins.then_inc(bn_done[n], 1)
                    after(dve, (bn_done[n], tile, 1, 1), own=True)
                    for g in range(TA):
                        ins = dve.bn_aggr(mv[n][:, g, :], bn[n][:, g, :])
                    ins.then_inc(stats[n], 1)

                def normalise(dst, src, n, r, signal):
                    for g in range(TA):
                        ins = dve.tensor_scalar(dst[:, g, :], src[:, g, :], mv[n][:, g, 0:1], r[:, g:g + 1],
                                                ALU.subtract, ALU.mult)
                    ins.then_inc(signal, 1)

                def work(*steps):
                    for kind, n in steps:
                        if kind == "mask" and live(b):
                            masks(n)
                        elif kind == "hidden" and live(m):
                            hidden_lo(m, n, h_hi, h_lo)

                if live(m):
                    after(dve, (scale["x2"], m, 2, 2), (res_ready, m, 1, 1))
                    normalise(X2, X2, "x2", rs["x2"], z2_ready)
                work(("mask", 0), ("mask", 1))
                if live(m):
                    lo_part(Z2T[1], Z2T[0], z2h, m, [(fc_ready, m - 1, 4, 4)], z2l)
                if live(e):
                    after(dve, (w2_ready, e, 1, 1), (x3b_ready, e, 1, 1), (stored, e - 1, 32, 32))
                    dve.tensor_tensor(OUTB[:].rearrange("p a c -> p (a c)"), rows[:, :], X3B[:].rearrange("p a c -> p (a c)"),
                                      ALU.add).then_inc(out_ready, 1)
                work(("mask", 2), ("mask", 3), ("mask", 4))
                if live(q):
                    lo_part(ZT[1], ZT[0], zh, q, [(vqk_ready, q - 1, 3, 3)], zl)
                if live(f):
                    after(dve, (scale["x3"], f, 2, 2), (z3_turned, f - 1, 1, 1))
                    normalise(Z3, X3, "x3", rs["x3"], z3_ready)
                work(("mask", 5), ("hidden", 0), ("mask", 6), ("mask", 7), ("hidden", 1), ("hidden", 2), ("hidden", 3))
                if peeled and i == 1:
                    bias(0)
                if peeled:
                    prepare(IN_MIDDLE.get(i, ()))
                if live(b):
                    statistics("xc", XC, b, xc_loaded, 32)
                if live(f):
                    lo_part(Z3T[1], Z3T[0], z3h, f, [(w1_ready, f - 1, 4, 4)], z3l)

                def elu(t):
                    after(dve, (qk_act, q, t + 1, 2))
                    dve.scalar_tensor_tensor(EXPRELU[:, t, :], EXPRELU[:, t, :], 1.0, EXPRELU[:, 2 + t, :],
                                             ALU.min, ALU.add).then_inc(qk_made, 1)

                if live(a):
                    statistics("x", X, a, x_loaded, 16)

                def invert(g):
                    after(dve, (den_moved, b, 64, 64))
                    dve.reciprocal(DD[:, 2 * g:2 * g + 2, :, :].rearrange("p j m t -> p (j m t)"),
                                   DD[:, 2 * g:2 * g + 2, :, :].rearrange("p j m t -> p (j m t)")).then_inc(den_inverted, 1)

                if live(q):
                    elu(0)
                if live(b):
                    invert(0)
                if live(q):
                    elu(1)
                if live(b):
                    invert(1)
                    for g in range(TA):
                        after(dve, (num_moved, b, 64, 64), (den_inverted, b, g + 1, 2), (at_hi, b - 1, 1, 1),
                              (at_lo, b - 1, 1, 1))
                        dve.tensor_tensor(AT[:, g, :, :].rearrange("p m (j t) -> p j m t", j=2), NN[:, 2 * g:2 * g + 2, :, :],
                                          DD[:, 2 * g:2 * g + 2, :, :], ALU.mult).then_inc(at_made, 1)
                if live(m):
                    after(dve, (proj_ready, m, 1, 1), (res_ready, m, 1, 1), (x3b_ready, m - 1, 1, 1), (z3_ready, m - 1, 1, 1))
                    dve.tensor_tensor(X3[:].rearrange("p a c -> p (a c)"), rows[:, :], RES[:].rearrange("p a c -> p (a c)"),
                                      ALU.add).then_inc(x3_ready, 1)
                if live(b):
                    after(dve, (scale["xc"], b, 2, 2), (x2_ready, b - 1, 1, 1))
                    normalise(Y, XC, "xc", rs["xc"], y_ready)
                    after(dve, (at_hi, b, 1, 1), (o_ready, b - 1, 1, 1))
                    dve.tensor_tensor(ATL[:].rearrange("p g m t -> p (g m t)"), AT[:].rearrange("p g m t -> p (g m t)"),
                                      ATH[:].rearrange("p g m t -> p (g m t)").bitcast(F32), ALU.subtract).then_inc(at_lo, 1)
                if live(q):
                    for t, moved in enumerate((q_moved, k_moved)):
                        after(dve, (qk_hi, q, t + 1, 2), (moved, q - 1, 96, 96))
                        dve.tensor_tensor(QKL[t][:, :, :].rearrange("p g n -> p (g n)"), EXPRELU[:, t, :],
                                          QKH[t][:, :, :].rearrange("p g n -> p (g n)").bitcast(F32),
                                          ALU.subtract).then_inc(qk_lo, 1)
                if live(f):
                    hidden_lo(f, 0, g_hi, g_lo)
                    hidden_lo(f, 1, g_hi, g_lo)
                if live(b):
                    after(dve, (o_ready, b, 1, 1), (yb_ready, b, 1, 1), (z2_turned, b - 1, 1, 1))
                    dve.tensor_tensor(X2[:].rearrange("p a c -> p (a c)"), rows[:, :], Y[:].rearrange("p a c -> p (a c)"),
                                      ALU.add).then_inc(x2_ready, 1)
                if live(b):
                    statistics("x2", X2, b, x2_ready, 1)
                if live(f):
                    hidden_lo(f, 2, g_hi, g_lo)
                    hidden_lo(f, 3, g_hi, g_lo)
                if live(m):
                    statistics("x3", X3, m, x3_ready, 1)
                if live(a):
                    after(dve, (scale["x"], a, 7, 7))
                    normalise(X, X, "x", rz, z_ready)

            run(dve, body)


def kernel(**inputs):
    import numpy as np
    import concourse.bacc as bacc
    from concourse.bass_utils import run_bass_kernel_spmd

    def channels(w, axis):
        w = np.moveaxis(np.asarray(w), axis, 0)
        w = w.reshape((H // 2, 2, D) + w.shape[1:])
        w = np.moveaxis(w, 0, 2).reshape((C,) + w.shape[3:])
        return np.ascontiguousarray(np.moveaxis(w, 0, axis))

    def columns(v):
        return np.ascontiguousarray(np.asarray(v).reshape(-1, P).T)

    g = lambda name: np.asarray(inputs["L0_" + name])
    qkv = ("q", "k", "v")
    r = np.arange(P)
    arrays = {
        "x": np.ascontiguousarray(g("attn_x").reshape(T, C)),
        "wqkv": np.ascontiguousarray(np.concatenate([channels(g(f"attn_{n}_w"), 0).T for n in qkv], axis=1)),
        "bqkv": np.ascontiguousarray(np.concatenate([columns(channels(g(f"attn_{n}_b"), 0)) for n in qkv], axis=1)),
        "ln1w": columns(g("attn_ln1_w")), "ln1b": columns(g("attn_ln1_b")),
        "wo": np.ascontiguousarray(channels(g("attn_o_w"), 1).T), "bo": g("attn_o_b"),
        "ln2w": columns(g("attn_ln2_w")), "ln2b": columns(g("attn_ln2_b")),
        "wfc": np.ascontiguousarray(g("attn_fc_w").T), "bfc": columns(g("attn_fc_b")),
        "wproj": np.ascontiguousarray(g("attn_proj_w").T), "bproj": g("attn_proj_b"),
        "w1": np.ascontiguousarray(g("ffn_W1")), "b1": columns(g("ffn_b1")),
        "w2": np.ascontiguousarray(g("ffn_W2")), "b2": g("ffn_b2"),
        "ident": np.eye(P, dtype=np.float32),
        "mask": (r[:, None] % CH == r[None, :] % CH).astype(np.float32),
    }
    nc = bacc.Bacc("TRN2", target_bir_lowering=False, num_devices=1)
    args = [nc.dram_tensor(f"in_{name}", a.shape, mybir.dt.from_np(a.dtype), kind="ExternalInput").ap() for name, a in arrays.items()]
    result = nc.dram_tensor("result", (T, C), F32, kind="ExternalOutput").ap()
    build(nc, *args, result)
    got = run_bass_kernel_spmd(nc, [{f"in_{n}": a for n, a in arrays.items()}], core_ids=[0])
    return got.results[0]["result"].reshape(8, T // 8, C)
```
